# Optimizing a Trainium2 kernel written in Bass

```python
import numpy as np
import jax
import jax.numpy as jnp

def _softmax(x, axis=-1):
    return jax.nn.softmax(x, axis=axis)

def _gelu(x):
    return jax.nn.gelu(x, approximate=True)

def _silu(x):
    return jax.nn.silu(x)

def _sigmoid(x):
    return jax.nn.sigmoid(x)

def _layernorm(x, axis=-1, eps=1e-05):
    m = jnp.mean(x, axis=axis, keepdims=True)
    v = jnp.var(x, axis=axis, keepdims=True)
    return (x - m) / jnp.sqrt(v + eps)

def _scatter_add(tgt, idx, src, axis=0):
    return tgt.at[idx].add(src)

def _segment_sum(src, seg, n):
    return jax.ops.segment_sum(src, seg, n)
kernel_name = 'mk_prb_d1_jaxref_r8_c7faed'

def setup_inputs(seed: int=0):
    np.random.seed(seed)
    _w = jnp.asarray

    def _L0_attn_setup():
        import jax, jax.numpy as jnp
        import numpy as np
        N_STATE = 64
        SEQ_L = 512
        BATCH, HCH = (16, 64)
        DT_MIN, DT_MAX = (0.001, 0.1)

        def _make_DPLR_HiPPO(N):
            P = np.sqrt(1 + 2 * np.arange(N))
            A = P[:, None] * P[None, :]
            A = np.tril(A) - np.diag(np.arange(N))
            nhippo = -A
            p = 0.5 * np.sqrt(2 * np.arange(1, N + 1) + 1.0)
            q = 2 * p
            S = nhippo + p[:, None] * q[None, :]
            Lambda, V = np.linalg.eig(S)
            Vc = V.conj().T
            p_t = Vc @ p
            q_t = Vc @ q.conj()
            return (Lambda, p_t, q_t, Vc)

        def _ri(z):
            return np.stack([z.real, z.imag], axis=-1).astype(np.float32)

        def _cplx(x_ri):
            return x_ri[..., 0] + 1j * x_ri[..., 1]

        def _s4_kernel(Lambda, p, q, B, Ct, step, L):
            Omega = jnp.exp(-2j * jnp.pi * (jnp.arange(L) / L))
            g = 2.0 / step * ((1.0 - Omega) / (1.0 + Omega))
            c = 2.0 / (1.0 + Omega)
            denom = g[:, None] - Lambda[None, :]
            cauchy = lambda v: (v[None, :] / denom).sum(-1)
            k00 = cauchy(Ct.conj() * B)
            k01 = cauchy(Ct.conj() * p)
            k10 = cauchy(q.conj() * B)
            k11 = cauchy(q.conj() * p)
            at_roots = c * (k00 - k01 * (1.0 / (1.0 + k11)) * k10)
            return jnp.fft.ifft(at_roots, L).real
        key = jax.random.key(seed)
        k_u, k_ct, k_b, k_d, k_ls = jax.random.split(key, 5)
        Lambda, p, q, Vc = _make_DPLR_HiPPO(N_STATE)
        u = jax.random.normal(k_u, (BATCH, HCH, SEQ_L), dtype=jnp.float32)
        Ct_ri = jax.random.normal(k_ct, (1, N_STATE, 2), dtype=jnp.float32) / np.sqrt(N_STATE)
        Bp = jax.random.normal(k_b, (N_STATE, 1), dtype=jnp.float32) / np.sqrt(N_STATE)
        D = jax.random.uniform(k_d, (1,), dtype=jnp.float32)
        log_step = jax.random.uniform(k_ls, (1,), dtype=jnp.float32, minval=np.log(DT_MIN), maxval=np.log(DT_MAX))
        return {'u': u, 'Lambda_ri': jnp.asarray(_ri(Lambda)), 'p_ri': jnp.asarray(_ri(p)), 'q_ri': jnp.asarray(_ri(q)), 'Vc_ri': jnp.asarray(_ri(Vc)), 'Ct_ri': Ct_ri, 'Bp': Bp, 'D': D, 'log_step': log_step}
    _L0_attn_in = _L0_attn_setup()

    def _L0_ffn_setup():
        import jax, jax.numpy as jnp
        import numpy as np
        BLOCK = 64
        NF4_CODE = jnp.array([-1.0, -0.6961928009986877, -0.5250730514526367, -0.39491748809814453, -0.28444138169288635, -0.18477343022823334, -0.09105003625154495, 0.0, 0.07958029955625534, 0.16093020141124725, 0.24611230194568634, 0.33791524171829224, 0.44070982933044434, 0.5626170039176941, 0.7229568362236023, 1.0], dtype=jnp.float32)

        def dequant_nf4(q, absmax, shape):
            w = NF4_CODE[q.reshape(-1)]
            w = w.reshape(-1, BLOCK) * absmax[:, None]
            return w.reshape(shape)
        key = jax.random.key(seed)
        ks = jax.random.split(key, 7)
        HD, M = (512, 1792)
        nblk = HD * M // BLOCK
        x = jax.random.normal(ks[0], (2, 256, HD), dtype=jnp.float32)
        gate_q = jax.random.randint(ks[1], (M, HD), 0, 16, dtype=jnp.int32)
        up_q = jax.random.randint(ks[2], (M, HD), 0, 16, dtype=jnp.int32)
        down_q = jax.random.randint(ks[3], (HD, M), 0, 16, dtype=jnp.int32)
        gate_absmax = jax.random.uniform(ks[4], (nblk,), dtype=jnp.float32) * 0.05
        up_absmax = jax.random.uniform(ks[5], (nblk,), dtype=jnp.float32) * 0.05
        down_absmax = jax.random.uniform(ks[6], (nblk,), dtype=jnp.float32) * 0.05
        return {'x': x, 'gate_q': gate_q, 'gate_absmax': gate_absmax, 'up_q': up_q, 'up_absmax': up_absmax, 'down_q': down_q, 'down_absmax': down_absmax}
    _L0_ffn_in = _L0_ffn_setup()
    _d = {'L0_attn_u': _L0_attn_in['u'], 'L0_attn_Lambda_ri': _L0_attn_in['Lambda_ri'], 'L0_attn_p_ri': _L0_attn_in['p_ri'], 'L0_attn_q_ri': _L0_attn_in['q_ri'], 'L0_attn_Vc_ri': _L0_attn_in['Vc_ri'], 'L0_attn_Ct_ri': _L0_attn_in['Ct_ri'], 'L0_attn_Bp': _L0_attn_in['Bp'], 'L0_attn_D': _L0_attn_in['D'], 'L0_attn_log_step': _L0_attn_in['log_step'], 'L0_ffn_gate_q': _L0_ffn_in['gate_q'], 'L0_ffn_gate_absmax': _L0_ffn_in['gate_absmax'], 'L0_ffn_up_q': _L0_ffn_in['up_q'], 'L0_ffn_up_absmax': _L0_ffn_in['up_absmax'], 'L0_ffn_down_q': _L0_ffn_in['down_q'], 'L0_ffn_down_absmax': _L0_ffn_in['down_absmax']}
    _x0 = _d['L0_attn_u']
    _d['L0_attn_u'] = jax.random.normal(jax.random.fold_in(jax.random.key(seed), 1), (4, 512, 512), dtype=_x0.dtype)
    del _x0
    return _d

def reference(L0_attn_u, L0_attn_Lambda_ri, L0_attn_p_ri, L0_attn_q_ri, L0_attn_Vc_ri, L0_attn_Ct_ri, L0_attn_Bp, L0_attn_D, L0_attn_log_step, L0_ffn_gate_q, L0_ffn_gate_absmax, L0_ffn_up_q, L0_ffn_up_absmax, L0_ffn_down_q, L0_ffn_down_absmax):

    def _L0_attn_ref(u, Lambda_ri, p_ri, q_ri, Vc_ri, Ct_ri, Bp, D, log_step):
        import jax, jax.numpy as jnp
        import numpy as np
        N_STATE = 64
        SEQ_L = 512
        BATCH, HCH = (16, 64)
        DT_MIN, DT_MAX = (0.001, 0.1)

        def _make_DPLR_HiPPO(N):
            P = np.sqrt(1 + 2 * np.arange(N))
            A = P[:, None] * P[None, :]
            A = np.tril(A) - np.diag(np.arange(N))
            nhippo = -A
            p = 0.5 * np.sqrt(2 * np.arange(1, N + 1) + 1.0)
            q = 2 * p
            S = nhippo + p[:, None] * q[None, :]
            Lambda, V = np.linalg.eig(S)
            Vc = V.conj().T
            p_t = Vc @ p
            q_t = Vc @ q.conj()
            return (Lambda, p_t, q_t, Vc)

        def _ri(z):
            return np.stack([z.real, z.imag], axis=-1).astype(np.float32)

        def _cplx(x_ri):
            return x_ri[..., 0] + 1j * x_ri[..., 1]

        def _s4_kernel(Lambda, p, q, B, Ct, step, L):
            Omega = jnp.exp(-2j * jnp.pi * (jnp.arange(L) / L))
            g = 2.0 / step * ((1.0 - Omega) / (1.0 + Omega))
            c = 2.0 / (1.0 + Omega)
            denom = g[:, None] - Lambda[None, :]
            cauchy = lambda v: (v[None, :] / denom).sum(-1)
            k00 = cauchy(Ct.conj() * B)
            k01 = cauchy(Ct.conj() * p)
            k10 = cauchy(q.conj() * B)
            k11 = cauchy(q.conj() * p)
            at_roots = c * (k00 - k01 * (1.0 / (1.0 + k11)) * k10)
            return jnp.fft.ifft(at_roots, L).real
        L = u.shape[-1]
        Lambda = _cplx(Lambda_ri)
        p = _cplx(p_ri)
        q = _cplx(q_ri)
        Vc = _cplx(Vc_ri)
        Ct = _cplx(Ct_ri).reshape(-1)
        B = (Vc @ Bp.astype(Vc.dtype)).reshape(-1)
        step = jnp.exp(log_step)[0]
        K = _s4_kernel(Lambda, p, q, B, Ct, step, L).astype(u.dtype)
        n = 2 * L
        y = jnp.fft.irfft(jnp.fft.rfft(u, n=n) * jnp.fft.rfft(K, n=n), n=n)[..., :L]
        return y + D[0] * u

    def _L0_ffn_ref(x, gate_q, gate_absmax, up_q, up_absmax, down_q, down_absmax):
        import jax, jax.numpy as jnp
        import numpy as np
        BLOCK = 64
        NF4_CODE = jnp.array([-1.0, -0.6961928009986877, -0.5250730514526367, -0.39491748809814453, -0.28444138169288635, -0.18477343022823334, -0.09105003625154495, 0.0, 0.07958029955625534, 0.16093020141124725, 0.24611230194568634, 0.33791524171829224, 0.44070982933044434, 0.5626170039176941, 0.7229568362236023, 1.0], dtype=jnp.float32)

        def dequant_nf4(q, absmax, shape):
            w = NF4_CODE[q.reshape(-1)]
            w = w.reshape(-1, BLOCK) * absmax[:, None]
            return w.reshape(shape)
        HD = x.shape[-1]
        M = gate_q.shape[0]
        Wg = dequant_nf4(gate_q, gate_absmax, (M, HD))
        Wu = dequant_nf4(up_q, up_absmax, (M, HD))
        Wd = dequant_nf4(down_q, down_absmax, (HD, M))
        g = jnp.einsum('bsh,mh->bsm', x, Wg)
        u = jnp.einsum('bsh,mh->bsm', x, Wu)
        h = jax.nn.silu(g) * u
        return jnp.einsum('bsm,hm->bsh', h, Wd)
    x = L0_attn_u
    xn = _layernorm(x, axis=-1)
    x = x + _L0_attn_ref(xn, L0_attn_Lambda_ri, L0_attn_p_ri, L0_attn_q_ri, L0_attn_Vc_ri, L0_attn_Ct_ri, L0_attn_Bp, L0_attn_D, L0_attn_log_step) + _L0_ffn_ref(xn, L0_ffn_gate_q, L0_ffn_gate_absmax, L0_ffn_up_q, L0_ffn_up_absmax, L0_ffn_down_q, L0_ffn_down_absmax)
    return x

_drawn_inputs = setup_inputs


def setup_inputs(seed=0):
    import zlib

    import numpy as np

    out = dict(_drawn_inputs(seed))
    spreads = {}
    factors = {'L0_attn_Lambda_ri': 8.0,
     'L0_attn_p_ri': 8.0,
     'L0_attn_q_ri': 8.0,
     'L0_attn_Vc_ri': 8.0,
     'L0_attn_Ct_ri': 8.0,
     'L0_attn_Bp': 8.0,
     'L0_ffn_gate_absmax': 3.802,
     'L0_ffn_up_absmax': 3.832,
     'L0_ffn_down_absmax': 3.833}
    for name, (base, spread) in spreads.items():
        noise = np.random.default_rng([zlib.crc32(name.encode()), seed]).standard_normal(out[name].shape)
        drawn = base * np.exp(spread * noise) if base else spread * noise
        out[name] = jnp.asarray(drawn.astype(out[name].dtype))
    for name, factor in factors.items():
        out[name] = (out[name] * factor).astype(out[name].dtype)
    return out
```

```python
from contextlib import ExitStack

import concourse.bass as bass
from concourse import mybir

P = 128
F32 = mybir.dt.float32
F16 = mybir.dt.float16
BF16 = mybir.dt.bfloat16
I32 = mybir.dt.int32
ALU = mybir.AluOpType
ACT = mybir.ActivationFunctionType
AX = mybir.AxisListType

TOKENS, HD, M = 2048, 512, 1792
NT = TOKENS // P
NC = HD // P
NM = M // P
CH = 512
NCH = TOKENS // CH
TPC = CH // P
NST = 64
EPS = 1e-5

GU = 2 * NM
AHEAD = 9
BEHIND = 6
STEPS = 8
RING = 4
HI, LO = 0, 1

NF4_PIVOT = -0.025715956464409828
NF4_LINES = [
    (0.09119964390993118, -0.6639638543128967),
    (0.09966794401407242, -0.7088291049003601),
    (0.08134990185499191, -0.5455029606819153),
    (0.0918029397726059, -0.6462011337280273),
    (0.1301555633544922, -0.8111001253128052),
    (0.12190717458724976, -0.9964603185653687),
    (0.30380719900131226, -1.025715947151184),
    (0.2770431935787201, -3.129931926727295),
]

XS = 2.0 ** 11
EXP_BITS = 0x7F800000
RSQRT_MAGIC = 0x5F3759DF


def ffn_conv_kernel(nc, x, q_gate, q_up, q_down, am_gate, am_up, am_down, am_flat, s4_cols, vct, bp,
                    d_skip, log_step, lines_b, root_rows, tab_rhs, tab_lhs, cos_cols, out):
    x_v = x.rearrange("b s d -> (b s) d").rearrange("(p t) d -> p t d", t=NT)
    out_v = out.rearrange("b s d -> (b s) d").rearrange("(p t) d -> p t d", t=NT)

    with ExitStack() as ctx:
        def sb(name, shape, dt):
            return ctx.enter_context(nc.sbuf_tensor(name, shape, dt))

        def sem(name):
            return ctx.enter_context(nc.semaphore(name))

        h = sb("h", [P, NM, 2, TOKENS], F16)
        xT = sb("xT", [P, NT, 2, NC, P], F16)
        wd = sb("wd", [P, NM, 2, HD], F16)
        w1 = sb("w1", [P, 2, 2, 2, NC, P], F16)
        line = sb("line", [P, RING, CH], F32)
        acc_l = sb("acc_l", [P, CH], F32)
        acc_r = sb("acc_r", [P, CH], F32)
        wt = sb("wt", [P, CH], F32)
        qs = sb("qs", [P, 2, CH], I32)
        am = sb("am", [P, 2, CH], F32)
        sil = sb("sil", [P, 2, CH], F32)
        ident = sb("ident", [P, P], F32)
        lb = sb("lb", [P, len(NF4_LINES)], F32)
        sc = sb("sc", [P, 24], F32)
        V = sb("V", [P, 2, 8], F32)
        cols = sb("cols", [P, 8], F32)
        yv = sb("yv", [P, 16], F32)
        at_s = sb("at_s", [P, 68], F32)

        def borrow(tensor_rows, shape, dt=F32):
            flat = tensor_rows.rearrange("p a b c -> p (a b c)")
            if dt != F16:
                flat = flat.bitcast(dt)
            return flat[:, 0:shape]

        xs = borrow(h[:, NM - 4:NM], NT * HD).rearrange("p (t d) -> p t d", t=NT)
        xnb = borrow(h[:, NM - 6:NM - 4], 8 * HD).rearrange("p (t d) -> p t d", t=8)
        misc = borrow(h[:, NM - 7:NM - 6], 2048)
        st6 = misc[:, 0:6 * NT].rearrange("p (t s) -> p t s", t=NT)
        mv = misc[:, 128:128 + 2 * NT].rearrange("p (t s) -> p t s", t=NT)
        rs = misc[:, 192:192 + 6 * NT].rearrange("p (k t) -> p k t", k=6)
        amf = misc[:, 320:320 + 3 * 112].rearrange("p (k n) -> p k n", k=3)
        amx = misc[:, 704:710]
        vcs = misc[0:NST, 736:736 + 2 * P]
        bps = misc[0:NST, 1000:1001]
        s4b = wd[:, 5:NM].rearrange("p m a b -> p (m a b)").bitcast(F32).rearrange("p (k n) -> p k n", k=NM - 5)
        rhs_t = s4b[:, 0:2].rearrange("p k (a f) -> p k a f", a=4)
        lhs_t = s4b[:, 2:4].rearrange("p k (a f) -> p k a f", a=4)
        roots = s4b[:, 4]
        e_re, e_im = s4b[:, 5, 0:256], s4b[:, 5, 256:512]
        e_m1, e_m2 = s4b[:, 6, 0:256], s4b[:, 6, 256:512]
        U = [s4b[:, k].rearrange("p (a f) -> p a f", a=4) for k in (4, 5, 6, 7)]
        T = s4b[:, 4]
        tz = wd[:, NM - 1]
        xr = w1.rearrange("p a b c d e -> p (a b c d e)").bitcast(F32).rearrange("p (t d) -> p t d", t=4)
        res = xT.rearrange("p t a c f -> p (t a c f)").bitcast(F32).rearrange("p (t d) -> p t d", t=NT)

        amax, pow2, inv2 = sc[:, 0:3], sc[:, 3:6], sc[:, 6:9]
        s_w = [sc[:, 9 + s:10 + s] for s in range(3)]
        c_gate, c_up, c_down, c_conv = (sc[:, k:k + 1] for k in (12, 13, 14, 15))
        kmax, kpow, kinv, s_k = (sc[:, k:k + 1] for k in (16, 17, 18, 19))
        two_over_step, d_col, lstep, krow = (sc[:, k:k + 1] for k in (20, 21, 22, 23))

        bank = [ctx.enter_context(nc.psum_tensor(f"bank{b}", [P, CH], F32)) for b in range(8)]

        q_ld = [sem(f"q_ld{b}") for b in range(2)]
        am_ld = [sem(f"am_ld{b}") for b in range(2)]
        x_ld = [sem(f"x_ld{c}") for c in range(NCH)]
        cst_ld = sem("cst_ld")
        amf_ld = sem("amf_ld")
        s4_ld = sem("s4_ld")
        tab_ld = sem("tab_ld")
        xr_ld = [sem(f"xr_ld{b}") for b in range(4)]
        out_st = sem("out_st")
        id_done = sem("id_done")
        line_done = sem("line_done")
        dq_done = sem("dq_done")
        whi_done = sem("whi_done")
        wlo_done = sem("wlo_done")
        sc_done = sem("sc_done")
        mx_done = sem("mx_done")
        ln_done = sem("ln_done")
        xn_done = sem("xn_done")
        tp_done = sem("tp_done")
        xhi_done = sem("xhi_done")
        xlo_done = sem("xlo_done")
        gate_done = sem("gate_done")
        up_done = sem("up_done")
        silu_done = sem("silu_done")
        h_done = sem("h_done")
        hhi_done = sem("hhi_done")
        hlo_done = sem("hlo_done")
        step_done = sem("step_done")
        b_mm = sem("b_mm")
        b_cp = sem("b_cp")
        v_done = sem("v_done")
        s4_done = sem("s4_done")
        inv_done = sem("inv_done")
        u_done = sem("u_done")
        t_done = sem("t_done")
        kmax_done = sem("kmax_done")
        tz_done = sem("tz_done")
        sum_done = sem("sum_done")
        toe_mm = sem("toe_mm")
        tri_done = sem("tri_done")
        conv_done = sem("conv_done")
        res_done = sem("res_done")
        down_done = sem("down_done")
        fin_done = sem("fin_done")

        V_STEPS = 17
        block = ctx.enter_context(nc.Block())

        @block.sync
        def _(sp):
            def load_unit(seq, slot, q_src, am_src, wait):
                if wait:
                    sp.wait_ge(line_done, 8 * (seq - 1))
                sp.dma_start(qs[:, slot, :], q_src).then_inc(q_ld[slot], 16)
                if wait:
                    sp.wait_ge(dq_done, STEPS * (seq - 1))
                for s in range(2):
                    sp.dma_start(am[64 * s:64 * s + 64, slot, :],
                                 am_src[s:s + 1, :].to_broadcast([64, CH])).then_inc(am_ld[slot], 16)

            def load_gu(mt, wait=True):
                load_unit(2 * mt, 0, q_gate[mt], am_gate[mt], wait)
                load_unit(2 * mt + 1, 1, q_up[mt], am_up[mt], wait)

            sp.dma_start(lb[:], lines_b).then_inc(cst_ld, 16)
            sp.dma_start(lstep, log_step.to_broadcast([P, 1])).then_inc(cst_ld, 16)
            sp.dma_start(d_col, d_skip.to_broadcast([P, 1])).then_inc(cst_ld, 16)
            load_unit(0, 0, q_gate[0], am_gate[0], False)
            sp.dma_start(cols[:], s4_cols).then_inc(s4_ld, 16)
            sp.dma_start(vcs, vct).then_inc(s4_ld, 16)
            sp.dma_start(bps, bp).then_inc(s4_ld, 16)
            for s in range(3):
                sp.dma_start(amf[:, s, :], am_flat[s]).then_inc(amf_ld, 16)
            sp.dma_start(xs[:, 0:TPC, :], x_v[:, 0:TPC, :]).then_inc(x_ld[0], 16)
            load_unit(1, 1, q_up[0], am_up[0], False)
            for c in range(1, NCH):
                sp.dma_start(xs[:, TPC * c:TPC * c + TPC, :], x_v[:, TPC * c:TPC * c + TPC, :]).then_inc(x_ld[c], 16)
            load_gu(1)
            sp.dma_start(rhs_t, tab_rhs).then_inc(tab_ld, 16)
            sp.dma_start(lhs_t, tab_lhs).then_inc(tab_ld, 16)
            sp.dma_start(roots, root_rows).then_inc(tab_ld, 16)
            sp.dma_start(at_s[:, 32:36], cos_cols).then_inc(tab_ld, 16)
            with sp.Fori(2, NM) as mt:
                load_gu(mt)
            load_unit(GU, 0, q_down[0], am_down[0], True)
            load_unit(GU + 1, 1, q_down[1], am_down[1], True)
            for t in range(4):
                sp.wait_ge(up_done, NCH * (NM - 1 + t // 2))
                sp.dma_start(xr[:, t, :], x_v[:, t, :]).then_inc(xr_ld[t], 16)
            for t in range(4, NT):
                sp.wait_ge(res_done, t - 3)
                sp.dma_start(xr[:, t % 4, :], x_v[:, t, :]).then_inc(xr_ld[t % 4], 16)
                if t in (7, 11):
                    mt = 2 + (t - 7) // 4
                    load_unit(GU + mt, mt % 2, q_down[mt], am_down[mt], True)
            with sp.Fori(4, NM - 1, 2) as mt:
                for par in range(2):
                    load_unit(GU + mt + par, par, q_down[mt + par], am_down[mt + par], True)
            for t in range(NT):
                sp.wait_ge(fin_done, t + 1)
                sp.dma_start(out_v[:, t, :], res[:, t, :]).then_inc(out_st, 16)
            sp.wait_ge(out_st, 16 * NT)

        @block.gpsimd
        def _(pool):
            pool.memset(ident[:], 0.0).then_inc(id_done, 1)
            pool.wait_ge(id_done, 1)
            pool.affine_select(out=ident[:], in_=ident[:], compare_op=ALU.not_equal, fill=1.0, base=0,
                               pattern=[[-1, P]], channel_multiplier=1).then_inc(id_done, 1)
            pool.wait_ge(sc_done, 1)
            pool.partition_all_reduce(amax, amx[:, 0:3], P, bass.bass_isa.ReduceOp.max).then_inc(mx_done, 1)

            pool.wait_ge(s4_ld, 48)
            pool.wait_ge(b_cp, 1)

            def chained(ins):
                ins.then_inc(v_done, 1)

            chained(pool.tensor_copy(yv[:, 4:6], cols[:, 0:2]))
            chained(pool.tensor_copy(yv[:, 2:3], yv[:, 1:2]))
            chained(pool.tensor_scalar(yv[:, 3:4], yv[:, 0:1], -1.0, None, ALU.mult))
            chained(pool.tensor_copy(yv[:, 6:7], cols[:, 1:2]))
            chained(pool.tensor_scalar(yv[:, 7:8], cols[:, 0:1], -1.0, None, ALU.mult))
            pool.wait_ge(v_done, 5)
            for i, a in enumerate((4, 2)):
                for j in range(2):
                    k = 2 * i + j
                    chained(pool.tensor_scalar(V[:, 0, 2 * k:2 * k + 2], yv[:, 4 * j:4 * j + 2],
                                               cols[:, a:a + 1], None, ALU.mult))
                    chained(pool.tensor_scalar(yv[:, 8 + 2 * k:10 + 2 * k], yv[:, 4 * j + 2:4 * j + 4],
                                               cols[:, a + 1:a + 2], None, ALU.mult))
            pool.wait_ge(v_done, 13)
            chained(pool.tensor_tensor(V[:, 0, :], V[:, 0, :], yv[:, 8:16], ALU.add))
            pool.wait_ge(v_done, 14)
            v0 = V[:, 0, :].rearrange("p (k c) -> p k c", c=2)
            v1 = V[:, 1, :].rearrange("p (k c) -> p k c", c=2)
            chained(pool.tensor_copy(v1[:, :, 0], v0[:, :, 1]))
            chained(pool.tensor_scalar(v1[:, :, 1], v0[:, :, 0], -1.0, None, ALU.mult))
            pool.wait_ge(v_done, 16)
            chained(pool.tensor_scalar(V[:, 0, :], V[:, 0, :], -1.0, None, ALU.mult))
            pool.wait_ge(t_done, 1)
            pool.affine_select(out=T[:, 0:P], in_=T[:, 0:P], compare_op=ALU.is_ge, fill=0.0, base=0,
                               pattern=[[1, P]], channel_multiplier=-1).then_inc(tri_done, 1)
            pool.wait_ge(t_done, 2)
            pool.partition_all_reduce(kmax, krow, P, bass.bass_isa.ReduceOp.max).then_inc(kmax_done, 1)

        @block.scalar
        def _(act):
            def make_line(seq, slot, loads, k):
                if k == 0:
                    act.wait_ge(q_ld[slot], 16 * loads)
                if not (isinstance(seq, int) and seq == 0 and k < RING):
                    act.wait_ge(dq_done, STEPS * (seq - 1) + 3 + k if k < RING else STEPS * seq + (k - 2) // 2)
                slope = NF4_LINES[k][0]
                nc.scalar.activation(line[:, k % RING, :], qs[:, slot, :], ACT.Identity, scale=slope,
                                     bias=lb[:, k:k + 1]).then_inc(line_done, 1)

            def weight_hi(seq, dst, free=None):
                act.wait_ge(dq_done, STEPS * (seq + 1))
                if free is not None:
                    act.wait_ge(up_done, free)
                nc.scalar.activation(dst, wt[:], ACT.Copy).then_inc(whi_done, 1)

            def items(mt, par, first, last):
                for p in range(first, last):
                    unit, i = p // 9, p % 9
                    if i != 4:
                        make_line(2 * mt + unit, unit % 2, mt + 1 + unit // 2, i if i < 4 else i - 1)
                        continue
                    before, buf = (mt - 1, 1 - par) if unit == 0 else (mt, par)
                    free = None if isinstance(before, int) and before < 2 else NCH * (before - 1)
                    which = (unit - 1) % 2
                    weight_hi(2 * mt + unit - 1, w1[:, buf, which, HI].rearrange("p c f -> p (c f)"), free)

            def down_items(mt, slot, loads, first, last):
                for i in range(first, last):
                    if i != 4:
                        make_line(GU + mt, slot, loads, i if i < 4 else i - 1)
                    else:
                        weight_hi(GU + mt - 1, wd[:, mt - 1, HI, :])

            def silu(k, c, pair):
                n = NCH * k + c
                act.wait_ge(gate_done, n + 1)
                if not (isinstance(k, int) and n < 2):
                    act.wait_ge(h_done, n - 1)
                nc.scalar.activation(sil[:, c % 2, :], bank[2 * pair][:], ACT.Silu,
                                     scale=c_gate).then_inc(silu_done, 1)

            def h_hi(k, c, pair):
                n = NCH * k + c
                act.wait_ge(h_done, n + 1)
                nc.scalar.activation(h[:, k, HI, CH * c:CH * c + CH], bank[2 * pair + 1][:],
                                     ACT.Copy).then_inc(hhi_done, 1)

            def x_hi(t):
                act.wait_ge(tp_done, t + 1)
                nc.scalar.activation(xT[:, t, HI].rearrange("p c f -> p (c f)"), bank[4 + t % 4][:],
                                     ACT.Copy).then_inc(xhi_done, 1)

            act.wait_ge(cst_ld, 48)
            nc.scalar.activation(lstep, lstep, ACT.Exp).then_inc(step_done, 1)
            items(0, 0, 0, 4)
            items(0, 0, 5, 14)
            for t in range(TPC):
                x_hi(t)
            act.wait_ge(b_mm, 1)
            nc.scalar.activation(yv[:, 0:2], bank[3][:, 0:2], ACT.Copy).then_inc(b_cp, 1)
            items(0, 0, 14, 18 + AHEAD)

            def window(k, par, pairs, with_x=False):
                for c in range(NCH):
                    silu(k, c, pairs[c])
                    items(k + 1, 1 - par, AHEAD + 18 * 2 * c // 8, AHEAD + 18 * (2 * c + 1) // 8)
                    if with_x and c + 1 < NCH:
                        for t in range(TPC * (c + 1), TPC * (c + 2)):
                            x_hi(t)
                    h_hi(k, c, pairs[c])
                    items(k + 1, 1 - par, AHEAD + 18 * (2 * c + 1) // 8, AHEAD + 18 * (2 * c + 2) // 8)

            window(0, 0, (0, 1, 0, 1), with_x=True)
            with act.Fori(1, NM - 2, 2) as k:
                window(k, 1, range(NCH))
                window(k + 1, 0, range(NCH))
            for c in range(NCH):
                silu(NM - 1, c, c)
                h_hi(NM - 1, c, c)
            down_items(0, 0, NM + 1, AHEAD, 9)
            for mt in range(1, 4):
                down_items(mt, mt % 2, NM + 1 + mt // 2, 0, 9)
            with act.Fori(2, NM // 2) as j:
                for par in range(2):
                    down_items(2 * j + par, par, NM + 1 + j, 0, 9)
            act.wait_ge(conv_done, NT)
            weight_hi(GU + NM - 1, wd[:, NM - 1, HI, :])

        @block.vector
        def _(dve):
            def step(seq, slot, loads, s_scale, s):
                made = 8 * seq
                if s == 0:
                    dve.wait_ge(line_done, made + 2)
                    ins = nc.vector.scalar_tensor_tensor(acc_l[:], line[:, 0, :], NF4_PIVOT, line[:, 1, :],
                                                         ALU.min, ALU.min)
                elif s == 1:
                    dve.wait_ge(line_done, made + 4)
                    ins = nc.vector.tensor_tensor(acc_r[:], line[:, 2, :], line[:, 3, :], ALU.max)
                elif s < 6:
                    dve.wait_ge(line_done, made + 3 + s)
                    dve.wait_ge(dq_done, STEPS * seq + s - 1)
                    acc, op = ((acc_l, ALU.min), (acc_r, ALU.max))[s % 2]
                    ins = nc.vector.tensor_tensor(acc[:], acc[:], line[:, (2 + s) % RING, :], op)
                elif s == 6:
                    dve.wait_ge(dq_done, STEPS * seq + 6)
                    ins = nc.vector.scalar_tensor_tensor(wt[:], acc_r[:], -NF4_PIVOT, acc_l[:],
                                                         ALU.max, ALU.add)
                else:
                    dve.wait_ge(am_ld[slot], 32 * loads)
                    dve.wait_ge(dq_done, STEPS * seq + 7)
                    ins = nc.vector.scalar_tensor_tensor(wt[:], wt[:], s_w[s_scale], am[:, slot, :],
                                                         ALU.mult, ALU.mult)
                ins.then_inc(dq_done, 1)

            def weight_lo(seq, hi, lo):
                dve.wait_ge(whi_done, seq + 1)
                nc.vector.tensor_tensor(lo, wt[:], hi, ALU.subtract).then_inc(wlo_done, 1)

            def items(mt, par, first, last):
                for p in range(first, last):
                    unit, i = p // 9, p % 9
                    if i != 2:
                        step(2 * mt + unit, unit % 2, mt + 1 + unit // 2, unit % 2, i if i < 2 else i - 1)
                        continue
                    buf = 1 - par if unit == 0 else par
                    w = w1[:, buf, (unit - 1) % 2].rearrange("p l c f -> p l (c f)")
                    weight_lo(2 * mt + unit - 1, w[:, HI, :], w[:, LO, :])

            def down_items(mt, slot, loads, first, last):
                for i in range(first, last):
                    if i != 2:
                        step(GU + mt, slot, loads, 2, i if i < 2 else i - 1)
                    else:
                        weight_lo(GU + mt - 1, wd[:, mt - 1, HI, :], wd[:, mt - 1, LO, :])

            def h_mul(k, c, pair):
                n = NCH * k + c
                dve.wait_ge(up_done, n + 1)
                dve.wait_ge(silu_done, n + 1)
                up = bank[2 * pair + 1]
                nc.vector.scalar_tensor_tensor(up[:], up[:], c_up, sil[:, c % 2, :],
                                               ALU.mult, ALU.mult).then_inc(h_done, 1)

            def h_lo(k, c, pair):
                n = NCH * k + c
                dve.wait_ge(hhi_done, n + 1)
                nc.vector.tensor_tensor(h[:, k, LO, CH * c:CH * c + CH].bitcast(BF16), bank[2 * pair + 1][:],
                                        h[:, k, HI, CH * c:CH * c + CH], ALU.subtract).then_inc(hlo_done, 1)

            sc_n = [0]

            def small(ins):
                ins.then_inc(sc_done, 1)
                sc_n[0] += 1
                dve.wait_ge(sc_done, sc_n[0])

            def exponent(maxima, power, inverse):
                small(nc.vector.tensor_scalar(maxima, maxima, 2.0 ** -40, None, ALU.max))
                small(nc.vector.tensor_scalar(power.bitcast(I32), maxima.bitcast(I32), EXP_BITS, None,
                                              ALU.bitwise_and))
                small(nc.vector.tensor_scalar(inverse.bitcast(I32), power.bitcast(I32), EXP_BITS, None,
                                              ALU.bitwise_xor))

            def scales():
                dve.wait_ge(mx_done, 1)
                exponent(amax, pow2, inv2)
                small(nc.vector.tensor_scalar(sc[:, 9:12], inv2, 2.0 ** 13, None, ALU.mult))
                small(nc.vector.tensor_scalar(c_gate, pow2[:, 0:1], 2.0 ** -14 / XS, None, ALU.mult))
                small(nc.vector.tensor_scalar(c_up, inv2[:, 0:1], 2.0 ** -6 * 2.0 ** -14 / XS, None, ALU.mult))
                small(nc.vector.tensor_scalar(c_down, pow2[:, 0:1], pow2[:, 1:2], 2.0 ** -9, ALU.mult, ALU.mult))
                small(nc.vector.tensor_scalar(c_down, c_down, pow2[:, 2:3], None, ALU.mult))

            ln_n = [0]

            def ln(ins):
                ins.then_inc(ln_done, 1)
                ln_n[0] += 1

            def ln_wait():
                dve.wait_ge(ln_done, ln_n[0])

            def stats(c):
                dve.wait_ge(x_ld[c], 16)
                tiles = range(TPC * c, TPC * c + TPC)
                for t in tiles:
                    ln(nc.vector.bn_stats(st6[:, t, :], xs[:, t, :]))
                ln_wait()
                for t in tiles:
                    ln(nc.vector.bn_aggr(mv[:, t, :], st6[:, t, :]))
                ln_wait()

            def rstd(a, b):
                v, hv, y, t = (rs[:, i, a:b] for i in range(4))
                ln(nc.vector.tensor_scalar(v, mv[:, a:b, 1], EPS, None, ALU.add))
                ln_wait()
                ln(nc.vector.tensor_scalar(hv, v, -0.5, None, ALU.mult))
                ln(nc.vector.tensor_scalar(t.bitcast(I32), v.bitcast(I32), 1, None, ALU.logical_shift_right))
                ln_wait()
                ln(nc.vector.tensor_scalar(y.bitcast(I32), t.bitcast(I32), -1.0, float(RSQRT_MAGIC),
                                           ALU.mult, ALU.add))
                ln_wait()
                for _ in range(4):
                    ln(nc.vector.tensor_tensor(t, y, y, ALU.mult))
                    ln_wait()
                    ln(nc.vector.tensor_tensor(t, t, hv, ALU.mult))
                    ln_wait()
                    ln(nc.vector.scalar_tensor_tensor(y, t, 1.5, y, ALU.add, ALU.mult))
                    ln_wait()
                ln(nc.vector.tensor_scalar(rs[:, 4, a:b], y, XS, None, ALU.mult))
                ln_wait()

            def norm(t):
                if t >= 8:
                    dve.wait_ge(tp_done, t - 7)
                nc.vector.tensor_scalar(xnb[:, t % 8, :], xs[:, t, :], mv[:, t, 0:1], rs[:, 4, t:t + 1],
                                        ALU.subtract, ALU.mult).then_inc(xn_done, 1)

            def x_lo(t):
                dve.wait_ge(xhi_done, t + 1)
                hi, lo = (xT[:, t, i].rearrange("p c f -> p (c f)") for i in (HI, LO))
                nc.vector.tensor_tensor(lo, bank[4 + t % 4][:], hi, ALU.subtract).then_inc(xlo_done, 1)

            dve.wait_ge(amf_ld, 48)
            nc.vector.tensor_reduce(amx[:, 0:3], amf, AX.X, ALU.max,
                                    apply_absolute_value=True).then_inc(sc_done, 1)
            sc_n[0] = 1
            items(0, 0, 0, 2)
            items(0, 0, 3, 8)
            scales()
            items(0, 0, 8, 9)
            stats(0)
            rstd(0, TPC)
            for t in range(TPC):
                norm(t)
            items(0, 0, 9, 12)
            for t in range(TPC):
                x_lo(t)
            items(0, 0, 12, 18 + BEHIND)

            def window(k, par, pairs, with_x=False):
                for c in range(NCH):
                    if with_x and c == 0:
                        for chunk in range(1, NCH):
                            stats(chunk)
                        rstd(TPC, NT)
                    if with_x and c + 1 < NCH:
                        for t in range(TPC * (c + 1), TPC * (c + 2)):
                            norm(t)
                    h_mul(k, c, pairs[c])
                    items(k + 1, 1 - par, BEHIND + 18 * 2 * c // 8, BEHIND + 18 * (2 * c + 1) // 8)
                    if with_x and c + 1 < NCH:
                        for t in range(TPC * (c + 1), TPC * (c + 2)):
                            x_lo(t)
                    h_lo(k, c, pairs[c])
                    items(k + 1, 1 - par, BEHIND + 18 * (2 * c + 1) // 8, BEHIND + 18 * (2 * c + 2) // 8)

            window(0, 0, (0, 1, 0, 1), with_x=True)
            with dve.Fori(1, NM - 2, 2) as k:
                window(k, 1, range(NCH))
                window(k + 1, 0, range(NCH))

            s4_n = [0]

            def s4(ins, wait=True):
                ins.then_inc(s4_done, 1)
                s4_n[0] += 1
                if wait:
                    dve.wait_ge(s4_done, s4_n[0])

            v = nc.vector
            last = NM - 1
            dve.wait_ge(tab_ld, 64)
            dve.wait_ge(s4_ld, 48)
            dve.wait_ge(step_done, 1)
            s4(v.reciprocal(two_over_step, lstep), False)
            s4(v.tensor_scalar(e_m1, roots[:, 0:256], cols[:, 7:8], None, ALU.mult))
            s4(v.tensor_scalar(two_over_step, two_over_step, 2.0, None, ALU.mult))
            s4(v.scalar_tensor_tensor(e_im, roots[:, 256:512], two_over_step, e_m1, ALU.mult, ALU.subtract), False)
            s4(v.tensor_scalar(e_re, roots[:, 0:256], cols[:, 6:7], None, ALU.mult))
            s4(v.tensor_tensor(e_m1, e_re, e_re, ALU.mult), False)
            s4(v.tensor_tensor(e_m2, e_im, e_im, ALU.mult))
            s4(v.tensor_tensor(e_m1, e_m1, e_m2, ALU.add))
            s4(v.reciprocal(e_m2, e_m1))
            v.tensor_tensor(e_re, e_re, e_m2, ALU.mult).then_inc(inv_done, 1)
            v.tensor_tensor(e_im, e_im, e_m2, ALU.mult).then_inc(inv_done, 1)
            h_mul(last, 0, 0)
            h_lo(last, 0, 0)
            dve.wait_ge(sum_done, 1)
            s4(v.tensor_copy(at_s[:, 0:16], bank[6][:, 0:16]), False)
            s4(v.tensor_copy(at_s[:, 16:32], bank[7][:, 16:32]))
            S = at_s[:, 0:32].rearrange("p (a k) -> p a k", a=4)
            cos_l = at_s[:, 32:36]
            s00, s01, s10, s11 = ((S[:, :, 2 * k], S[:, :, 2 * k + 1]) for k in range(4))
            nr, ni, dr, di, t0, t1, t2, t3 = (at_s[:, 36 + 4 * i:40 + 4 * i] for i in range(8))
            s4(v.tensor_tensor(nr, s01[0], s10[0], ALU.mult), False)
            s4(v.tensor_tensor(t0, s01[1], s10[1], ALU.mult), False)
            s4(v.tensor_tensor(ni, s01[0], s10[1], ALU.mult), False)
            s4(v.tensor_tensor(t1, s01[1], s10[0], ALU.mult), False)
            s4(v.tensor_tensor(dr, cos_l, s11[0], ALU.mult), False)
            s4(v.tensor_tensor(di, cos_l, s11[1], ALU.mult))
            s4(v.tensor_tensor(nr, nr, t0, ALU.subtract), False)
            s4(v.tensor_tensor(ni, ni, t1, ALU.add), False)
            s4(v.tensor_scalar(dr, dr, 1.0, None, ALU.add))
            s4(v.tensor_tensor(t0, dr, dr, ALU.mult), False)
            s4(v.tensor_tensor(t1, di, di, ALU.mult))
            s4(v.tensor_tensor(t0, t0, t1, ALU.add))
            s4(v.reciprocal(t1, t0))
            s4(v.tensor_tensor(t2, t1, cos_l, ALU.mult))
            s4(v.tensor_tensor(nr, nr, t2, ALU.mult), False)
            s4(v.tensor_tensor(ni, ni, t2, ALU.mult))
            s4(v.tensor_tensor(t0, nr, dr, ALU.mult), False)
            s4(v.tensor_tensor(t1, ni, di, ALU.mult))
            s4(v.tensor_tensor(t0, t0, t1, ALU.add), False)
            s4(v.tensor_tensor(t3, ni, dr, ALU.mult), False)
            s4(v.tensor_tensor(t2, nr, di, ALU.mult))
            s4(v.tensor_tensor(t1, t3, t2, ALU.subtract))
            s4(v.tensor_tensor(nr, s00[0], t0, ALU.subtract), False)
            s4(v.tensor_tensor(ni, s00[1], t1, ALU.subtract))
            for a in range(4):
                s4(v.tensor_scalar(U[2][:, a, :], lhs_t[:, 1, a, :], ni[:, a:a + 1], None, ALU.mult), False)
                s4(v.tensor_scalar(U[3][:, a, :], lhs_t[:, 1, a, :], nr[:, a:a + 1], None, ALU.mult), False)
            dve.wait_ge(s4_done, s4_n[0])
            for a in range(4):
                s4(v.scalar_tensor_tensor(U[0][:, a, :], lhs_t[:, 0, a, :], nr[:, a:a + 1], U[2][:, a, :],
                                          ALU.mult, ALU.subtract), False)
                s4(v.scalar_tensor_tensor(U[1][:, a, :], lhs_t[:, 0, a, :], ni[:, a:a + 1], U[3][:, a, :],
                                          ALU.mult, ALU.add), False)
            dve.wait_ge(s4_done, s4_n[0])
            v.tensor_scalar(s4b[:, 6], s4b[:, 4], -1.0, None, ALU.mult).then_inc(u_done, 1)
            v.tensor_scalar(s4b[:, 7], s4b[:, 5], -1.0, None, ALU.mult).then_inc(u_done, 1)
            h_mul(last, 1, 1)
            h_lo(last, 1, 1)
            h_mul(last, 2, 2)
            h_lo(last, 2, 2)
            dve.wait_ge(toe_mm, 1)
            v.tensor_copy(T, bank[0][:]).then_inc(t_done, 1)
            dve.wait_ge(tri_done, 1)
            s4(v.scalar_tensor_tensor(T[:, 0:P], ident[:], d_col, T[:, 0:P], ALU.mult, ALU.add))
            v.tensor_reduce(krow, T, AX.X, ALU.max, apply_absolute_value=True).then_inc(t_done, 1)
            dve.wait_ge(kmax_done, 1)
            exponent(kmax, kpow, kinv)
            small(v.tensor_scalar(s_k, kinv, 2.0 ** 13, None, ALU.mult))
            small(v.tensor_scalar(c_conv, kpow, 2.0 ** -14 / XS, None, ALU.mult))
            s4(v.tensor_scalar(tz[:, HI, :], T, s_k, None, ALU.mult))
            v.scalar_tensor_tensor(tz[:, LO, :], T, s_k, tz[:, HI, :], ALU.mult, ALU.subtract).then_inc(tz_done, 1)
            h_mul(last, 3, 3)
            h_lo(last, 3, 3)

            for t in range(NT):
                for p in range(BEHIND + (36 - BEHIND) * t // NT, BEHIND + (36 - BEHIND) * (t + 1) // NT):
                    mt = p // 9
                    down_items(mt, mt % 2, NM + 1 + mt // 2, p % 9, p % 9 + 1)
                dve.wait_ge(conv_done, t + 1)
                dve.wait_ge(xr_ld[t % 4], 16 * (t // 4 + 1))
                v.scalar_tensor_tensor(res[:, t, :], bank[t % 4][:], c_conv, xr[:, t % 4, :],
                                       ALU.mult, ALU.add).then_inc(res_done, 1)
            with dve.Fori(2, NM // 2) as j:
                for par in range(2):
                    down_items(2 * j + par, par, NM + 1 + j, 0, 9)
            weight_lo(GU + NM - 1, wd[:, NM - 1, HI, :], wd[:, NM - 1, LO, :])
            for t in range(NT):
                dve.wait_ge(down_done, t + 1)
                v.scalar_tensor_tensor(res[:, t, :], bank[(t + 4) % 8][:], c_down, res[:, t, :],
                                       ALU.mult, ALU.add).then_inc(fin_done, 1)

        @block.tensor
        def _(pe):
            def transpose_tile(t):
                pe.wait_ge(xn_done, t + 1)
                if t >= 4:
                    pe.wait_ge(xlo_done, t - 3)
                for c in range(NC):
                    mm = nc.tensor.transpose(bank[4 + t % 4][:, P * c:P * c + P],
                                             xnb[:, t % 8, P * c:P * c + P], ident[:])
                mm.then_inc(tp_done, 1)

            def products(k, par, c, pair):
                for unit, done in ((0, gate_done), (1, up_done)):
                    if c == 0:
                        pe.wait_ge(wlo_done, 2 * k + unit + 1)
                    out_b = bank[2 * pair + unit]
                    n = 0
                    for f in range(NC):
                        for wl, xl in ((HI, HI), (HI, LO), (LO, HI)):
                            mm = nc.tensor.matmul(out_b[:], w1[:, par, unit, wl, f, :],
                                                  xT[:, TPC * c:TPC * c + TPC, xl, f, :],
                                                  start=(n == 0), stop=(n == 3 * NC - 1))
                            n += 1
                    mm.then_inc(done, 1)

            pe.wait_ge(s4_ld, 48)
            for i in range(2):
                mm = nc.tensor.matmul(bank[3][:, i:i + 1], vcs[:, P * i:P * i + P], bps, start=True, stop=True)
            mm.then_inc(b_mm, 1)
            pe.wait_ge(id_done, 2)
            for t in range(TPC):
                transpose_tile(t)
            for c in range(NCH):
                if c >= 2:
                    pe.wait_ge(hlo_done, c - 1)
                if c == 1:
                    pe.wait_ge(b_cp, 1)
                pe.wait_ge(xlo_done, TPC * (c + 1))
                products(0, 0, c, c % 2)
                if c + 1 < NCH:
                    for t in range(TPC * (c + 1), TPC * (c + 2)):
                        transpose_tile(t)

            def window(k, par):
                for c in range(NCH):
                    if isinstance(k, int) and k == 1:
                        if c < 2:
                            pe.wait_ge(hlo_done, 3 + c)
                    else:
                        pe.wait_ge(hlo_done, NCH * k + c - 3)
                    products(k, par, c, c)

            window(1, 1)
            with pe.Fori(2, NM - 3, 2) as k:
                window(k, 0)
                window(k + 1, 1)
            window(NM - 2, 0)

            last = NM - 1
            n0 = NCH * last
            pe.wait_ge(hlo_done, n0 - 3)
            products(last, 1, 0, 0)
            pe.wait_ge(hlo_done, n0)
            pe.wait_ge(v_done, V_STEPS)
            pe.wait_ge(inv_done, 2)
            for a in range(4):
                rows = slice(64 * (a // 2), 64 * (a // 2) + 64)
                f = P * (a % 2)
                sums = bank[6 + a // 2][:, 8 * a:8 * a + 8]
                nc.tensor.matmul(sums, e_re[rows, f:f + P], V[rows, 0, :],
                                 start=True, stop=False)
                mm = nc.tensor.matmul(sums, e_im[rows, f:f + P], V[rows, 1, :],
                                      start=False, stop=True)
            mm.then_inc(sum_done, 1)
            products(last, 1, 1, 1)
            products(last, 1, 2, 2)
            pe.wait_ge(u_done, 2)
            pe.wait_ge(hlo_done, n0 + 1)
            terms = (((0, 0), (3, 1)), ((2, 1), (3, 0)), ((2, 0), (1, 1)), ((0, 1), (1, 0)))
            for b in range(4):
                n = 0
                for a in range(4):
                    for u, cs in terms[a * b % 4]:
                        mm = nc.tensor.matmul(bank[0][:, P * b:P * b + P], U[u][:, a, :], rhs_t[:, cs, a, :],
                                              start=(n == 0), stop=(n == 7))
                        n += 1
            mm.then_inc(toe_mm, 1)
            products(last, 1, 3, 3)

            pe.wait_ge(tz_done, 1)
            pe.wait_ge(hlo_done, n0 + 2)
            for t in range(NT):
                if t >= 4:
                    pe.wait_ge(res_done, t - 3)
                n = 0
                for j in range(NC):
                    for xl, tl in ((HI, HI), (HI, LO), (LO, HI)):
                        mm = nc.tensor.matmul(bank[t % 4][:, P * j:HD], xT[:, t, xl, j, :],
                                              tz[:, tl, 0:HD - P * j], start=(n == 0), stop=(n == 3 * NC - 1))
                        n += 1
                mm.then_inc(conv_done, 1)

            def down(mt, group):
                for i in range(8):
                    t = 8 * group + i
                    if isinstance(mt, int) and mt == 0:
                        if t == 4:
                            pe.wait_ge(res_done, NT)
                        if t >= 8:
                            pe.wait_ge(fin_done, t - 7)
                    for n, (hl, wl) in enumerate(((HI, HI), (HI, LO), (LO, HI))):
                        part = h[:, mt, hl, P * t:P * t + P]
                        if hl == LO:
                            part = part.bitcast(BF16)
                        mm = nc.tensor.matmul(bank[(t + 4) % 8][:], part, wd[:, mt, wl, :],
                                              start=(isinstance(mt, int) and mt == 0 and n == 0),
                                              stop=(isinstance(mt, int) and mt == NM - 1 and n == 2))
                    if isinstance(mt, int) and mt == NM - 1:
                        mm.then_inc(down_done, 1)

            pe.wait_ge(hlo_done, NCH * NM)
            for group in range(2):
                pe.wait_ge(wlo_done, GU + 1)
                down(0, group)
                with pe.Fori(1, NM - 1) as mt:
                    pe.wait_ge(wlo_done, GU + 1 + mt)
                    down(mt, group)
                pe.wait_ge(wlo_done, GU + NM)
                down(NM - 1, group)


def _s4_tables(np):
    L = HD
    p, a, f = np.arange(P)[:, None, None], np.arange(4)[None, :, None], np.arange(P)[None, None, :]
    root = 4 * p + a
    rhs = 2 * np.pi * (root * f % L) / L
    lhs = np.pi * (root * (1 - 2 * f) % (2 * L)) / L
    rows = (4 * np.arange(P)[None, :] + np.arange(4)[:, None]).reshape(2, 256) * np.pi / L
    rows = np.repeat(rows, NST, axis=0)
    f32 = np.float32
    return (np.concatenate([np.cos(rows), np.sin(rows)], axis=1).astype(f32),
            np.stack([np.cos(rhs), np.sin(rhs)], axis=1).reshape(P, 2, 4, P).astype(f32),
            (np.stack([np.cos(lhs), np.sin(lhs)], axis=1) / L).reshape(P, 2, 4, P).astype(f32),
            np.cos(root[:, :, 0] * np.pi / L).astype(f32))


def kernel(**inputs):
    import numpy as np
    import concourse.bacc as bacc
    from concourse.bass_utils import run_bass_kernel_spmd

    i = {k: np.asarray(v) for k, v in inputs.items()}

    def gu_codes(q):
        return q.reshape(NM, P, NC, P).transpose(0, 3, 2, 1).reshape(NM, P, HD)

    def gu_absmax(am):
        return am.reshape(NM, P, NC, 2).transpose(0, 3, 2, 1).reshape(NM, 2, HD)

    vc = i["L0_attn_Vc_ri"].transpose(1, 2, 0)
    cols = np.concatenate([i["L0_attn_p_ri"], i["L0_attn_q_ri"], i["L0_attn_Ct_ri"].reshape(NST, 2),
                           i["L0_attn_Lambda_ri"]], axis=1)
    root_rows, tab_rhs, tab_lhs, cos_cols = _s4_tables(np)
    flat = np.stack([i["L0_ffn_gate_absmax"], i["L0_ffn_up_absmax"], i["L0_ffn_down_absmax"]])
    arrays = {
        "x": i["L0_attn_u"],
        "q_gate": gu_codes(i["L0_ffn_gate_q"]),
        "q_up": gu_codes(i["L0_ffn_up_q"]),
        "q_down": i["L0_ffn_down_q"].reshape(HD, NM, P).transpose(1, 2, 0),
        "am_gate": gu_absmax(i["L0_ffn_gate_absmax"]),
        "am_up": gu_absmax(i["L0_ffn_up_absmax"]),
        "am_down": i["L0_ffn_down_absmax"].reshape(HD, NM, 2).transpose(1, 2, 0),
        "am_flat": flat.reshape(3, P, HD * M // 64 // P),
        "s4_cols": np.concatenate([cols, cols], axis=0),
        "vct": np.concatenate([vc, vc], axis=2).reshape(NST, 2 * P),
        "bp": i["L0_attn_Bp"],
        "d_skip": i["L0_attn_D"].reshape(1, 1),
        "log_step": i["L0_attn_log_step"].reshape(1, 1),
        "lines_b": np.tile(np.array([b for _, b in NF4_LINES], np.float32), (P, 1)),
        "root_rows": root_rows,
        "tab_rhs": tab_rhs,
        "tab_lhs": tab_lhs,
        "cos_cols": cos_cols,
    }
    arrays = {f"in_{k}": np.ascontiguousarray(a) for k, a in arrays.items()}

    nc = bacc.Bacc("TRN2", target_bir_lowering=False, num_devices=1)
    args = [nc.dram_tensor(k, a.shape, mybir.dt.from_np(a.dtype), kind="ExternalInput").ap()
            for k, a in arrays.items()]
    args.append(nc.dram_tensor("out_0", i["L0_attn_u"].shape, F32, kind="ExternalOutput").ap())
    ffn_conv_kernel(nc, *args)
    r = run_bass_kernel_spmd(nc, [arrays], core_ids=[0])
    return r.results[0]["out_0"]
```

```python
from contextlib import ExitStack

import concourse.bass as bass
from concourse import mybir

P = 128
F32 = mybir.dt.float32
F16 = mybir.dt.float16
BF16 = mybir.dt.bfloat16
I32 = mybir.dt.int32
ALU = mybir.AluOpType
ACT = mybir.ActivationFunctionType
AX = mybir.AxisListType

TOKENS, HD, M = 2048, 512, 1792
NT = TOKENS // P
NC = HD // P
NM = M // P
CH = 512
NCH = TOKENS // CH
TPC = CH // P
NST = 64
EPS = 1e-5

GU = 2 * NM
AHEAD = 9
BEHIND = 6
STEPS = 8
RING = 4
CONV_END = 45
DOWN_LOOP = 6
HI, LO = 0, 1

NF4_PIVOT = -0.025715956464409828
NF4_LINES = [
    (0.09119964390993118, -0.6639638543128967),
    (0.09966794401407242, -0.7088291049003601),
    (0.08134990185499191, -0.5455029606819153),
    (0.0918029397726059, -0.6462011337280273),
    (0.1301555633544922, -0.8111001253128052),
    (0.12190717458724976, -0.9964603185653687),
    (0.30380719900131226, -1.025715947151184),
    (0.2770431935787201, -3.129931926727295),
]

XS = 2.0 ** 11
EXP_BITS = 0x7F800000
RSQRT_MAGIC = 0x5F3759DF


def ffn_conv_kernel(nc, x, q_gate, q_up, q_down, am_gate, am_up, am_down, am_flat, s4_cols, vct, bp,
                    d_skip, log_step, lines_b, root_rows, tab_rhs, tab_lhs, cos_cols, out):
    x_v = x.rearrange("b s d -> (b s) d").rearrange("(p t) d -> p t d", t=NT)
    out_v = out.rearrange("b s d -> (b s) d").rearrange("(p t) d -> p t d", t=NT)

    with ExitStack() as ctx:
        def sb(name, shape, dt):
            return ctx.enter_context(nc.sbuf_tensor(name, shape, dt))

        def sem(name):
            return ctx.enter_context(nc.semaphore(name))

        h = sb("h", [P, NM, 2, TOKENS], F16)
        xT = sb("xT", [P, NT, 2, NC, P], F16)
        wd = sb("wd", [P, NM, 2, HD], F16)
        w1 = sb("w1", [P, 2, 2, 2, NC, P], F16)
        line = sb("line", [P, RING, CH], F32)
        acc_l = sb("acc_l", [P, CH], F32)
        acc_r = sb("acc_r", [P, CH], F32)
        wt = sb("wt", [P, CH], F32)
        qs = sb("qs", [P, 2, CH], I32)
        am = sb("am", [P, 2, CH], F32)
        sil = sb("sil", [P, 2, CH], F32)
        ident = sb("ident", [P, P], F32)
        lb = sb("lb", [P, len(NF4_LINES)], F32)
        sc = sb("sc", [P, 24], F32)
        V = sb("V", [P, 2, 8], F32)
        cols = sb("cols", [P, 8], F32)
        yv = sb("yv", [P, 16], F32)
        at_s = sb("at_s", [P, 68], F32)

        def borrow(tensor_rows, shape, dt=F32):
            flat = tensor_rows.rearrange("p a b c -> p (a b c)")
            if dt != F16:
                flat = flat.bitcast(dt)
            return flat[:, 0:shape]

        xs = borrow(h[:, NM - 4:NM], NT * HD).rearrange("p (t d) -> p t d", t=NT)
        xnb = borrow(h[:, NM - 6:NM - 4], 8 * HD).rearrange("p (t d) -> p t d", t=8)
        misc = borrow(h[:, NM - 7:NM - 6], 2048)
        st6 = misc[:, 0:6 * NT].rearrange("p (t s) -> p t s", t=NT)
        mv = misc[:, 128:128 + 2 * NT].rearrange("p (t s) -> p t s", t=NT)
        rs = misc[:, 192:192 + 6 * NT].rearrange("p (k t) -> p k t", k=6)
        amf = misc[:, 320:320 + 3 * 112].rearrange("p (k n) -> p k n", k=3)
        amx = misc[:, 704:710]
        vcs = misc[0:NST, 736:736 + 2 * P]
        bps = misc[0:NST, 1000:1001]
        s4b = wd[:, 5:NM].rearrange("p m a b -> p (m a b)").bitcast(F32).rearrange("p (k n) -> p k n", k=NM - 5)
        rhs_t = s4b[:, 0:2].rearrange("p k (a f) -> p k a f", a=4)
        lhs_t = s4b[:, 2:4].rearrange("p k (a f) -> p k a f", a=4)
        roots = s4b[:, 4]
        e_re, e_im = s4b[:, 5, 0:256], s4b[:, 5, 256:512]
        e_m1, e_m2 = s4b[:, 6, 0:256], s4b[:, 6, 256:512]
        U = [s4b[:, k].rearrange("p (a f) -> p a f", a=4) for k in (4, 5, 6, 7)]
        T = s4b[:, 4]
        tz = wd[:, NM - 1]
        xr = w1.rearrange("p a b c d e -> p (a b c d e)").bitcast(F32).rearrange("p (t d) -> p t d", t=4)
        res = xT.rearrange("p t a c f -> p (t a c f)").bitcast(F32).rearrange("p (t d) -> p t d", t=NT)

        amax, pow2, inv2 = sc[:, 0:3], sc[:, 3:6], sc[:, 6:9]
        s_w = [sc[:, 9 + s:10 + s] for s in range(3)]
        c_gate, c_up, c_down, c_conv = (sc[:, k:k + 1] for k in (12, 13, 14, 15))
        kmax, kpow, kinv, s_k = (sc[:, k:k + 1] for k in (16, 17, 18, 19))
        two_over_step, d_col, lstep, krow = (sc[:, k:k + 1] for k in (20, 21, 22, 23))

        bank = [ctx.enter_context(nc.psum_tensor(f"bank{b}", [P, CH], F32)) for b in range(8)]

        q_ld = [sem(f"q_ld{b}") for b in range(2)]
        am_ld = [sem(f"am_ld{b}") for b in range(2)]
        x0_ld = [sem(f"x0_ld{t}") for t in range(TPC)]
        x_ld = [sem(f"x_ld{c}") for c in range(1, NCH)]
        lb_ld = sem("lb_ld")
        cst_ld = sem("cst_ld")
        amf_ld = sem("amf_ld")
        s4_ld = sem("s4_ld")
        tab_ld = sem("tab_ld")
        xr_ld = [sem(f"xr_ld{b}") for b in range(4)]
        out_st = sem("out_st")
        id_done = sem("id_done")
        line_done = sem("line_done")
        dq_done = sem("dq_done")
        whi_done = sem("whi_done")
        wlo_done = sem("wlo_done")
        sc_done = sem("sc_done")
        mx_done = sem("mx_done")
        ln_done = sem("ln_done")
        xn_done = sem("xn_done")
        tp_done = sem("tp_done")
        xhi_done = sem("xhi_done")
        xlo_done = sem("xlo_done")
        gate_done = sem("gate_done")
        up_done = sem("up_done")
        silu_done = sem("silu_done")
        h_done = sem("h_done")
        hhi_done = sem("hhi_done")
        hlo_done = sem("hlo_done")
        step_done = sem("step_done")
        b_mm = sem("b_mm")
        b_cp = sem("b_cp")
        v_done = sem("v_done")
        s4_done = sem("s4_done")
        inv_done = sem("inv_done")
        u_done = sem("u_done")
        t_done = sem("t_done")
        kmax_done = sem("kmax_done")
        tz_done = sem("tz_done")
        sum_done = sem("sum_done")
        toe_mm = sem("toe_mm")
        tri_done = sem("tri_done")
        conv_done = sem("conv_done")
        res_done = sem("res_done")
        down_done = sem("down_done")
        fin_done = sem("fin_done")

        SUMS_READ = 11
        V_STEPS = 17
        block = ctx.enter_context(nc.Block())

        @block.sync
        def _(sp):
            def load_absmax(slot, am_src):
                for s in range(2):
                    sp.dma_start(am[64 * s:64 * s + 64, slot, :],
                                 am_src[s:s + 1, :].to_broadcast([64, CH])).then_inc(am_ld[slot], 16)

            def load_unit(seq, slot, q_src, am_src, wait):
                if wait:
                    sp.wait_ge(line_done, 8 * (seq - 1))
                sp.dma_start(qs[:, slot, :], q_src).then_inc(q_ld[slot], 16)
                if wait:
                    sp.wait_ge(dq_done, STEPS * (seq - 1))
                load_absmax(slot, am_src)

            def load_gu(mt, wait=True):
                load_unit(2 * mt, 0, q_gate[mt], am_gate[mt], wait)
                load_unit(2 * mt + 1, 1, q_up[mt], am_up[mt], wait)

            sp.dma_start(lb[:], lines_b).then_inc(lb_ld, 16)
            sp.dma_start(qs[:, 0, :], q_gate[0]).then_inc(q_ld[0], 16)
            for s in range(3):
                sp.dma_start(amf[:, s, :], am_flat[s]).then_inc(amf_ld, 16)
            for t in range(TPC):
                sp.dma_start(xs[:, t, :], x_v[:, t, :]).then_inc(x0_ld[t], 16)
            load_absmax(0, am_gate[0])
            load_unit(1, 1, q_up[0], am_up[0], False)
            sp.dma_start(lstep, log_step.to_broadcast([P, 1])).then_inc(cst_ld, 16)
            sp.dma_start(d_col, d_skip.to_broadcast([P, 1])).then_inc(cst_ld, 16)
            for c in range(1, NCH):
                sp.dma_start(xs[:, TPC * c:TPC * c + TPC, :],
                             x_v[:, TPC * c:TPC * c + TPC, :]).then_inc(x_ld[c - 1], 16)
                if c == 1:
                    sp.dma_start(cols[:], s4_cols).then_inc(s4_ld, 16)
                    sp.dma_start(vcs, vct).then_inc(s4_ld, 16)
                    sp.dma_start(bps, bp).then_inc(s4_ld, 16)
            load_gu(1)
            sp.dma_start(rhs_t, tab_rhs).then_inc(tab_ld, 16)
            sp.dma_start(lhs_t, tab_lhs).then_inc(tab_ld, 16)
            sp.dma_start(roots, root_rows).then_inc(tab_ld, 16)
            sp.dma_start(at_s[:, 32:36], cos_cols).then_inc(tab_ld, 16)
            with sp.Fori(2, NM) as mt:
                load_gu(mt)
            def load_down(mt, par):
                load_unit(GU + mt, par, q_down[mt], am_down[mt], True)

            for mt in range(4):
                load_down(mt, mt % 2)
            for t in range(NT):
                if t < 4:
                    sp.wait_ge(up_done, NCH * (NM - 1 + t // 2))
                else:
                    sp.wait_ge(res_done, t - 3)
                sp.dma_start(xr[:, t % 4, :], x_v[:, t, :]).then_inc(xr_ld[t % 4], 16)
                if t in (3, 12):
                    load_down(4 + t // 12, t // 12)
            with sp.Fori(DOWN_LOOP, NM - 1, 2) as mt:
                for par in range(2):
                    load_down(mt + par, par)
            for t in range(NT):
                sp.wait_ge(fin_done, t + 1)
                sp.dma_start(out_v[:, t, :], res[:, t, :]).then_inc(out_st, 16)
            sp.wait_ge(out_st, 16 * NT)

        @block.gpsimd
        def _(pool):
            pool.memset(ident[:], 0.0).then_inc(id_done, 1)
            pool.wait_ge(id_done, 1)
            pool.affine_select(out=ident[:], in_=ident[:], compare_op=ALU.not_equal, fill=1.0, base=0,
                               pattern=[[-1, P]], channel_multiplier=1).then_inc(id_done, 1)
            pool.wait_ge(sc_done, 1)
            pool.partition_all_reduce(amax, amx[:, 0:3], P, bass.bass_isa.ReduceOp.max).then_inc(mx_done, 1)

            pool.wait_ge(s4_ld, 48)
            pool.wait_ge(b_cp, 1)

            def chained(ins):
                ins.then_inc(v_done, 1)

            chained(pool.tensor_copy(yv[:, 4:6], cols[:, 0:2]))
            chained(pool.tensor_copy(yv[:, 2:3], yv[:, 1:2]))
            chained(pool.tensor_scalar(yv[:, 3:4], yv[:, 0:1], -1.0, None, ALU.mult))
            chained(pool.tensor_copy(yv[:, 6:7], cols[:, 1:2]))
            chained(pool.tensor_scalar(yv[:, 7:8], cols[:, 0:1], -1.0, None, ALU.mult))
            pool.wait_ge(v_done, 5)
            for i, a in enumerate((4, 2)):
                for j in range(2):
                    k = 2 * i + j
                    chained(pool.tensor_scalar(V[:, 0, 2 * k:2 * k + 2], yv[:, 4 * j:4 * j + 2],
                                               cols[:, a:a + 1], None, ALU.mult))
                    chained(pool.tensor_scalar(yv[:, 8 + 2 * k:10 + 2 * k], yv[:, 4 * j + 2:4 * j + 4],
                                               cols[:, a + 1:a + 2], None, ALU.mult))
            pool.wait_ge(v_done, 13)
            chained(pool.tensor_tensor(V[:, 0, :], V[:, 0, :], yv[:, 8:16], ALU.add))
            pool.wait_ge(v_done, 14)
            v0 = V[:, 0, :].rearrange("p (k c) -> p k c", c=2)
            v1 = V[:, 1, :].rearrange("p (k c) -> p k c", c=2)
            chained(pool.tensor_copy(v1[:, :, 0], v0[:, :, 1]))
            chained(pool.tensor_scalar(v1[:, :, 1], v0[:, :, 0], -1.0, None, ALU.mult))
            pool.wait_ge(v_done, 16)
            chained(pool.tensor_scalar(V[:, 0, :], V[:, 0, :], -1.0, None, ALU.mult))
            pool.wait_ge(t_done, 1)
            pool.affine_select(out=T[:, 0:P], in_=T[:, 0:P], compare_op=ALU.is_ge, fill=0.0, base=0,
                               pattern=[[1, P]], channel_multiplier=-1).then_inc(tri_done, 1)
            pool.wait_ge(t_done, 2)
            pool.partition_all_reduce(kmax, krow, P, bass.bass_isa.ReduceOp.max).then_inc(kmax_done, 1)

        @block.scalar
        def _(act):
            def make_line(seq, slot, loads, k):
                if k == 0:
                    act.wait_ge(q_ld[slot], 16 * loads)
                if not (isinstance(seq, int) and seq == 0 and k < RING):
                    act.wait_ge(dq_done, STEPS * (seq - 1) + 3 + k if k < RING else STEPS * seq + (k - 2) // 2)
                slope = NF4_LINES[k][0]
                nc.scalar.activation(line[:, k % RING, :], qs[:, slot, :], ACT.Identity, scale=slope,
                                     bias=lb[:, k:k + 1]).then_inc(line_done, 1)

            def weight_hi(seq, dst, free=None):
                act.wait_ge(dq_done, STEPS * (seq + 1))
                if free is not None:
                    act.wait_ge(up_done, free)
                nc.scalar.activation(dst, wt[:], ACT.Copy).then_inc(whi_done, 1)

            def items(mt, par, first, last):
                for p in range(first, last):
                    unit, i = p // 9, p % 9
                    if i != 4:
                        make_line(2 * mt + unit, unit % 2, mt + 1 + unit // 2, i if i < 4 else i - 1)
                        continue
                    before, buf = mt + (unit - 1) // 2, (par + (unit - 1) // 2) % 2
                    free = None if isinstance(before, int) and before < 2 else NCH * (before - 1)
                    which = (unit - 1) % 2
                    weight_hi(2 * mt + unit - 1, w1[:, buf, which, HI].rearrange("p c f -> p (c f)"), free)

            def down_unit(mt, slot, loads, first, last):
                for i in range(first, last):
                    if i != 4:
                        make_line(GU + mt, slot, loads, i if i < 4 else i - 1)
                    else:
                        weight_hi(GU + mt - 1, wd[:, mt - 1, HI, :])

            def down_items(first, last):
                for p in range(first, last):
                    mt = p // 9
                    down_unit(mt, mt % 2, NM + 1 + mt // 2, p % 9, p % 9 + 1)

            def silu(k, c, pair):
                n = NCH * k + c
                act.wait_ge(gate_done, n + 1)
                if not (isinstance(k, int) and n < 2):
                    act.wait_ge(h_done, n - 1)
                nc.scalar.activation(sil[:, c % 2, :], bank[2 * pair][:], ACT.Silu,
                                     scale=c_gate).then_inc(silu_done, 1)

            def h_hi(k, c, pair):
                n = NCH * k + c
                act.wait_ge(h_done, n + 1)
                nc.scalar.activation(h[:, k, HI, CH * c:CH * c + CH], bank[2 * pair + 1][:],
                                     ACT.Copy).then_inc(hhi_done, 1)

            def x_hi(c):
                for t in range(TPC * c, TPC * c + TPC):
                    act.wait_ge(tp_done, t + 1)
                    nc.scalar.activation(xT[:, t, HI].rearrange("p c f -> p (c f)"), bank[4 + t % 4][:],
                                         ACT.Copy).then_inc(xhi_done, 1)

            def window(k, par):
                for c in range(NCH):
                    silu(k, c, c)
                    items(k + 1, 1 - par, AHEAD + 18 * 2 * c // 8, AHEAD + 18 * (2 * c + 1) // 8)
                    h_hi(k, c, c)
                    items(k + 1, 1 - par, AHEAD + 18 * (2 * c + 1) // 8, AHEAD + 18 * (2 * c + 2) // 8)

            act.wait_ge(lb_ld, 16)
            items(0, 0, 0, 4)
            items(0, 0, 5, 14)
            x_hi(0)
            items(0, 0, 14, 23)
            act.wait_ge(cst_ld, 32)
            nc.scalar.activation(lstep, lstep, ACT.Exp).then_inc(step_done, 1)
            act.wait_ge(b_mm, 1)
            nc.scalar.activation(yv[:, 0:2], bank[3][:, 0:2], ACT.Copy).then_inc(b_cp, 1)
            x_hi(1)
            items(0, 0, 23, 29)
            silu(0, 0, 0)
            x_hi(2)
            h_hi(0, 0, 0)
            items(0, 0, 29, 33)
            silu(0, 1, 1)
            h_hi(0, 1, 1)
            x_hi(3)
            items(0, 0, 33, 37)
            silu(0, 2, 0)
            items(0, 0, 37, 39)
            h_hi(0, 2, 0)
            items(0, 0, 39, 41)
            silu(0, 3, 1)
            items(0, 0, 41, 43)
            h_hi(0, 3, 1)
            items(0, 0, 43, 36 + AHEAD)
            with act.Fori(1, NM - 2, 2) as k:
                window(k, 1)
                window(k + 1, 0)
            for c in range(NCH):
                silu(NM - 1, c, c)
                down_items(AHEAD + 18 * 2 * c // 8, AHEAD + 18 * (2 * c + 1) // 8)
                h_hi(NM - 1, c, c)
                down_items(AHEAD + 18 * (2 * c + 1) // 8, AHEAD + 18 * (2 * c + 2) // 8)
            down_items(18 + AHEAD, 9 * DOWN_LOOP)
            with act.Fori(DOWN_LOOP // 2, NM // 2) as j:
                for par in range(2):
                    down_unit(2 * j + par, par, NM + 1 + j, 0, 9)
            act.wait_ge(conv_done, NT)
            weight_hi(GU + NM - 1, wd[:, NM - 1, HI, :])

        @block.vector
        def _(dve):
            def step(seq, slot, loads, s_scale, s):
                made = 8 * seq
                if s == 0:
                    dve.wait_ge(line_done, made + 2)
                    ins = nc.vector.scalar_tensor_tensor(acc_l[:], line[:, 0, :], NF4_PIVOT, line[:, 1, :],
                                                         ALU.min, ALU.min)
                elif s == 1:
                    dve.wait_ge(line_done, made + 4)
                    ins = nc.vector.tensor_tensor(acc_r[:], line[:, 2, :], line[:, 3, :], ALU.max)
                elif s < 6:
                    dve.wait_ge(line_done, made + 3 + s)
                    dve.wait_ge(dq_done, STEPS * seq + s - 1)
                    acc, op = ((acc_l, ALU.min), (acc_r, ALU.max))[s % 2]
                    ins = nc.vector.tensor_tensor(acc[:], acc[:], line[:, (2 + s) % RING, :], op)
                elif s == 6:
                    dve.wait_ge(dq_done, STEPS * seq + 6)
                    ins = nc.vector.scalar_tensor_tensor(wt[:], acc_r[:], -NF4_PIVOT, acc_l[:],
                                                         ALU.max, ALU.add)
                else:
                    dve.wait_ge(am_ld[slot], 32 * loads)
                    dve.wait_ge(dq_done, STEPS * seq + 7)
                    ins = nc.vector.scalar_tensor_tensor(wt[:], wt[:], s_w[s_scale], am[:, slot, :],
                                                         ALU.mult, ALU.mult)
                ins.then_inc(dq_done, 1)

            def weight_lo(seq, hi, lo):
                dve.wait_ge(whi_done, seq + 1)
                nc.vector.tensor_tensor(lo, wt[:], hi, ALU.subtract).then_inc(wlo_done, 1)

            def items(mt, par, first, last):
                for p in range(first, last):
                    unit, i = p // 9, p % 9
                    if i != 2:
                        step(2 * mt + unit, unit % 2, mt + 1 + unit // 2, unit % 2, i if i < 2 else i - 1)
                        continue
                    buf = (par + (unit - 1) // 2) % 2
                    w = w1[:, buf, (unit - 1) % 2].rearrange("p l c f -> p l (c f)")
                    weight_lo(2 * mt + unit - 1, w[:, HI, :], w[:, LO, :])

            def down_unit(mt, slot, loads, first, last):
                for i in range(first, last):
                    if i != 2:
                        step(GU + mt, slot, loads, 2, i if i < 2 else i - 1)
                    else:
                        weight_lo(GU + mt - 1, wd[:, mt - 1, HI, :], wd[:, mt - 1, LO, :])

            def down_items(first, last):
                for p in range(first, last):
                    mt = p // 9
                    down_unit(mt, mt % 2, NM + 1 + mt // 2, p % 9, p % 9 + 1)

            def h_mul(k, c, pair):
                n = NCH * k + c
                dve.wait_ge(up_done, n + 1)
                dve.wait_ge(silu_done, n + 1)
                up = bank[2 * pair + 1]
                nc.vector.scalar_tensor_tensor(up[:], up[:], c_up, sil[:, c % 2, :],
                                               ALU.mult, ALU.mult).then_inc(h_done, 1)

            def h_lo(k, c, pair):
                n = NCH * k + c
                dve.wait_ge(hhi_done, n + 1)
                nc.vector.tensor_tensor(h[:, k, LO, CH * c:CH * c + CH].bitcast(BF16), bank[2 * pair + 1][:],
                                        h[:, k, HI, CH * c:CH * c + CH], ALU.subtract).then_inc(hlo_done, 1)

            sc_n = [0]

            def small(op, *args, **kw):
                dve.wait_ge(sc_done, sc_n[0])
                op(*args, **kw).then_inc(sc_done, 1)
                sc_n[0] += 1

            def exponent(s, maxima, power, inverse):
                if s == 0:
                    small(nc.vector.tensor_scalar, maxima, maxima, 2.0 ** -40, None, ALU.max)
                elif s == 1:
                    small(nc.vector.tensor_scalar, power.bitcast(I32), maxima.bitcast(I32), EXP_BITS, None,
                          ALU.bitwise_and)
                else:
                    small(nc.vector.tensor_scalar, inverse.bitcast(I32), power.bitcast(I32), EXP_BITS, None,
                          ALU.bitwise_xor)

            SCALES = 8

            def scales(s):
                if s == 0:
                    dve.wait_ge(mx_done, 1)
                if s < 3:
                    exponent(s, amax, pow2, inv2)
                elif s == 3:
                    small(nc.vector.tensor_scalar, sc[:, 9:12], inv2, 2.0 ** 13, None, ALU.mult)
                elif s == 4:
                    small(nc.vector.tensor_scalar, c_gate, pow2[:, 0:1], 2.0 ** -14 / XS, None, ALU.mult)
                elif s == 5:
                    small(nc.vector.tensor_scalar, c_up, inv2[:, 0:1], 2.0 ** -6 * 2.0 ** -14 / XS, None, ALU.mult)
                elif s == 6:
                    small(nc.vector.tensor_scalar, c_down, pow2[:, 0:1], pow2[:, 1:2], 2.0 ** -9, ALU.mult, ALU.mult)
                else:
                    small(nc.vector.tensor_scalar, c_down, c_down, pow2[:, 2:3], None, ALU.mult)

            ln_n = [0]

            def ln(op, *args, wait=True, **kw):
                if wait:
                    dve.wait_ge(ln_done, ln_n[0])
                op(*args, **kw).then_inc(ln_done, 1)
                ln_n[0] += 1

            def stats(t):
                if t < TPC:
                    dve.wait_ge(x0_ld[t], 16)
                else:
                    dve.wait_ge(x_ld[t // TPC - 1], 16)
                ln(nc.vector.bn_stats, st6[:, t, :], xs[:, t, :], wait=False)

            def moments(c):
                dve.wait_ge(ln_done, ln_n[0])
                for t in range(TPC * c, TPC * c + TPC):
                    ln(nc.vector.bn_aggr, mv[:, t, :], st6[:, t, :], wait=False)

            RSTD = 14

            def rstd(c, s):
                a, b = TPC * c, TPC * c + TPC
                v, hv, y, t = (rs[:, i, a:b] for i in range(4))
                if s == 0:
                    ln(nc.vector.tensor_scalar, v, mv[:, a:b, 1], EPS, None, ALU.add)
                elif s == 1:
                    ln(nc.vector.tensor_scalar, hv, v, -0.5, None, ALU.mult)
                elif s == 2:
                    ln(nc.vector.tensor_scalar, t.bitcast(I32), v.bitcast(I32), 1, None,
                       ALU.logical_shift_right, wait=False)
                elif s == 3:
                    ln(nc.vector.tensor_scalar, y.bitcast(I32), t.bitcast(I32), -1.0, float(RSQRT_MAGIC),
                       ALU.mult, ALU.add)
                elif s == RSTD - 1:
                    ln(nc.vector.tensor_scalar, rs[:, 4, a:b], y, XS, None, ALU.mult)
                elif s % 3 == 1:
                    ln(nc.vector.tensor_tensor, t, y, y, ALU.mult)
                elif s % 3 == 2:
                    ln(nc.vector.tensor_tensor, t, t, hv, ALU.mult)
                else:
                    ln(nc.vector.scalar_tensor_tensor, y, t, 1.5, y, ALU.add, ALU.mult)

            def norm(c):
                dve.wait_ge(ln_done, ln_n[0])
                for t in range(TPC * c, TPC * c + TPC):
                    if t >= 8:
                        dve.wait_ge(tp_done, t - 7)
                    nc.vector.tensor_scalar(xnb[:, t % 8, :], xs[:, t, :], mv[:, t, 0:1], rs[:, 4, t:t + 1],
                                            ALU.subtract, ALU.mult).then_inc(xn_done, 1)

            def x_lo(c):
                for t in range(TPC * c, TPC * c + TPC):
                    dve.wait_ge(xhi_done, t + 1)
                    hi, lo = (xT[:, t, i].rearrange("p c f -> p (c f)") for i in (HI, LO))
                    nc.vector.tensor_tensor(lo, bank[4 + t % 4][:], hi, ALU.subtract).then_inc(xlo_done, 1)

            def layer_norm(c, first, last):
                for t in range(TPC * c, TPC * c + TPC):
                    stats(t)
                moments(c)
                spread = last - first
                for s in range(RSTD):
                    rstd(c, s)
                    items(0, 0, first + spread * s // RSTD, first + spread * (s + 1) // RSTD)
                norm(c)

            dve.wait_ge(amf_ld, 48)
            nc.vector.tensor_reduce(amx[:, 0:3], amf, AX.X, ALU.max,
                                    apply_absolute_value=True).then_inc(sc_done, 1)
            sc_n[0] = 1
            items(0, 0, 0, 2)
            for t in range(TPC):
                scales(2 * t)
                stats(t)
                scales(2 * t + 1)
                items(0, 0, 3 + t, 4 + t)
            moments(0)
            dve.wait_ge(sc_done, 1 + SCALES)
            for s in range(RSTD):
                rstd(0, s)
                if s % 7 == 3:
                    items(0, 0, 7 + s // 7, 8 + s // 7)
            norm(0)
            items(0, 0, 9, 12)
            x_lo(0)
            layer_norm(1, 12, 18)
            items(0, 0, 18, 21)
            x_lo(1)
            layer_norm(2, 21, 25)
            h_mul(0, 0, 0)
            items(0, 0, 25, 27)
            h_lo(0, 0, 0)
            x_lo(2)
            layer_norm(3, 27, 29)
            h_mul(0, 1, 1)
            items(0, 0, 29, 31)
            h_lo(0, 1, 1)
            x_lo(3)
            items(0, 0, 31, 34)
            h_mul(0, 2, 0)
            items(0, 0, 34, 36)
            h_lo(0, 2, 0)
            items(0, 0, 36, 38)
            h_mul(0, 3, 1)
            items(0, 0, 38, 40)
            h_lo(0, 3, 1)
            items(0, 0, 40, 36 + BEHIND)

            def window(k, par, stage=None):
                for c in range(NCH):
                    h_mul(k, c, c)
                    items(k + 1, 1 - par, BEHIND + 18 * 2 * c // 8, BEHIND + 18 * (2 * c + 1) // 8)
                    if stage:
                        stage(2 * c)
                    h_lo(k, c, c)
                    items(k + 1, 1 - par, BEHIND + 18 * (2 * c + 1) // 8, BEHIND + 18 * (2 * c + 2) // 8)
                    if stage:
                        stage(2 * c + 1)

            with dve.Fori(1, NM - 6, 2) as k:
                window(k, 1)
                window(k + 1, 0)

            v = nc.vector
            s4_n, s4_wait = [0], [False]

            def s4(op, *args, more=False, done=s4_done):
                if s4_wait[0]:
                    dve.wait_ge(s4_done, s4_n[0])
                op(*args).then_inc(done, 1)
                s4_n[0] += done is s4_done
                s4_wait[0] = not more

            def inverse_e(s):
                if s == 0:
                    dve.wait_ge(tab_ld, 64)
                    dve.wait_ge(s4_ld, 48)
                    dve.wait_ge(step_done, 1)
                    s4(v.reciprocal, two_over_step, lstep, more=True)
                    s4(v.tensor_scalar, e_m1, roots[:, 0:256], cols[:, 7:8], None, ALU.mult)
                elif s == 1:
                    s4(v.tensor_scalar, two_over_step, two_over_step, 2.0, None, ALU.mult)
                    s4(v.scalar_tensor_tensor, e_im, roots[:, 256:512], two_over_step, e_m1,
                       ALU.mult, ALU.subtract, more=True)
                elif s == 2:
                    s4(v.tensor_scalar, e_re, roots[:, 0:256], cols[:, 6:7], None, ALU.mult)
                    s4(v.tensor_tensor, e_m1, e_re, e_re, ALU.mult, more=True)
                elif s == 3:
                    s4(v.tensor_tensor, e_m2, e_im, e_im, ALU.mult)
                    s4(v.tensor_tensor, e_m1, e_m1, e_m2, ALU.add)
                elif s == 4:
                    s4(v.reciprocal, e_m2, e_m1)
                elif s == 5:
                    s4(v.tensor_tensor, e_re, e_re, e_m2, ALU.mult, more=True, done=inv_done)
                    s4(v.tensor_tensor, e_im, e_im, e_m2, ALU.mult, more=True, done=inv_done)

            S = at_s[:, 0:32].rearrange("p (a k) -> p a k", a=4)
            cos_l = at_s[:, 32:36]
            s00, s01, s10, s11 = ((S[:, :, 2 * k], S[:, :, 2 * k + 1]) for k in range(4))
            nr, ni, dr, di, t0, t1, t2, t3 = (at_s[:, 36 + 4 * i:40 + 4 * i] for i in range(8))

            def at_roots(s):
                if s == 0:
                    dve.wait_ge(sum_done, 1)
                    s4(v.tensor_copy, at_s[:, 0:16], bank[6][:, 0:16], more=True)
                    s4(v.tensor_copy, at_s[:, 16:32], bank[7][:, 16:32])
                elif s == 1:
                    s4(v.tensor_tensor, nr, s01[0], s10[0], ALU.mult, more=True)
                    s4(v.tensor_tensor, t0, s01[1], s10[1], ALU.mult, more=True)
                    s4(v.tensor_tensor, ni, s01[0], s10[1], ALU.mult, more=True)
                    s4(v.tensor_tensor, t1, s01[1], s10[0], ALU.mult, more=True)
                    s4(v.tensor_tensor, dr, cos_l, s11[0], ALU.mult, more=True)
                    s4(v.tensor_tensor, di, cos_l, s11[1], ALU.mult)
                    s4(v.tensor_tensor, nr, nr, t0, ALU.subtract, more=True)
                    s4(v.tensor_tensor, ni, ni, t1, ALU.add, more=True)
                elif s == 2:
                    s4(v.tensor_scalar, dr, dr, 1.0, None, ALU.add)
                    s4(v.tensor_tensor, t0, dr, dr, ALU.mult, more=True)
                    s4(v.tensor_tensor, t1, di, di, ALU.mult)
                    s4(v.tensor_tensor, t0, t0, t1, ALU.add)
                elif s == 3:
                    s4(v.reciprocal, t1, t0)
                    s4(v.tensor_tensor, t2, t1, cos_l, ALU.mult)
                    s4(v.tensor_tensor, nr, nr, t2, ALU.mult, more=True)
                    s4(v.tensor_tensor, ni, ni, t2, ALU.mult)
                else:
                    s4(v.tensor_tensor, t0, nr, dr, ALU.mult, more=True)
                    s4(v.tensor_tensor, t1, ni, di, ALU.mult)
                    s4(v.tensor_tensor, t0, t0, t1, ALU.add, more=True)
                    s4(v.tensor_tensor, t3, ni, dr, ALU.mult, more=True)
                    s4(v.tensor_tensor, t2, nr, di, ALU.mult)
                    s4(v.tensor_tensor, t1, t3, t2, ALU.subtract)
                    s4(v.tensor_tensor, nr, s00[0], t0, ALU.subtract, more=True)
                    s4(v.tensor_tensor, ni, s00[1], t1, ALU.subtract)

            def u_rows(s):
                if s < 2:
                    for a in range(2 * s, 2 * s + 2):
                        s4(v.tensor_scalar, U[2][:, a, :], lhs_t[:, 1, a, :], ni[:, a:a + 1], None, ALU.mult,
                           more=True)
                        s4(v.tensor_scalar, U[3][:, a, :], lhs_t[:, 1, a, :], nr[:, a:a + 1], None, ALU.mult,
                           more=(a < 3))
                elif s == 2:
                    for a in range(4):
                        s4(v.scalar_tensor_tensor, U[0][:, a, :], lhs_t[:, 0, a, :], nr[:, a:a + 1],
                           U[2][:, a, :], ALU.mult, ALU.subtract, more=True)
                        s4(v.scalar_tensor_tensor, U[1][:, a, :], lhs_t[:, 0, a, :], ni[:, a:a + 1],
                           U[3][:, a, :], ALU.mult, ALU.add, more=(a < 3))
                else:
                    s4(v.tensor_scalar, s4b[:, 6], s4b[:, 4], -1.0, None, ALU.mult, more=True, done=u_done)
                    s4(v.tensor_scalar, s4b[:, 7], s4b[:, 5], -1.0, None, ALU.mult, more=True, done=u_done)

            def toeplitz(s):
                if s == 0:
                    dve.wait_ge(toe_mm, 1)
                    v.tensor_copy(T, bank[6][:]).then_inc(t_done, 1)
                elif s == 1:
                    dve.wait_ge(tri_done, 1)
                    s4(v.scalar_tensor_tensor, T[:, 0:P], ident[:], d_col, T[:, 0:P], ALU.mult, ALU.add)
                elif s == 2:
                    dve.wait_ge(s4_done, s4_n[0])
                    v.tensor_reduce(krow, T, AX.X, ALU.max, apply_absolute_value=True).then_inc(t_done, 1)
                elif s == 3:
                    dve.wait_ge(kmax_done, 1)
                    for i in range(3):
                        exponent(i, kmax, kpow, kinv)
                    small(v.tensor_scalar, s_k, kinv, 2.0 ** 13, None, ALU.mult)
                    small(v.tensor_scalar, c_conv, kpow, 2.0 ** -14 / XS, None, ALU.mult)
                else:
                    dve.wait_ge(sc_done, sc_n[0])
                    s4(v.tensor_scalar, tz[:, HI, :], T, s_k, None, ALU.mult)
                    s4(v.scalar_tensor_tensor, tz[:, LO, :], T, s_k, tz[:, HI, :], ALU.mult, ALU.subtract,
                       done=tz_done)

            def roots_stage(slot):
                if 2 <= slot < 7:
                    at_roots(slot - 2)

            def rows_stage(slot):
                if slot % 2 == 0:
                    u_rows(slot // 2)

            def toeplitz_stage(slot):
                if 2 <= slot < 7:
                    toeplitz(slot - 2)

            window(NM - 5, 1, stage=inverse_e)
            window(NM - 4, 0, stage=roots_stage)
            window(NM - 3, 1, stage=rows_stage)
            window(NM - 2, 0, stage=toeplitz_stage)
            for c in range(NCH):
                h_mul(NM - 1, c, c)
                down_items(BEHIND + 18 * 2 * c // 8, BEHIND + 18 * (2 * c + 1) // 8)
                h_lo(NM - 1, c, c)
                down_items(BEHIND + 18 * (2 * c + 1) // 8, BEHIND + 18 * (2 * c + 2) // 8)

            for t in range(NT):
                d0 = 18 + BEHIND
                down_items(d0 + (CONV_END - d0) * t // NT, d0 + (CONV_END - d0) * (t + 1) // NT)
                dve.wait_ge(conv_done, t + 1)
                dve.wait_ge(xr_ld[t % 4], 16 * (t // 4 + 1))
                v.scalar_tensor_tensor(res[:, t, :], bank[t % 4][:], c_conv, xr[:, t % 4, :],
                                       ALU.mult, ALU.add).then_inc(res_done, 1)
            down_items(CONV_END, 9 * DOWN_LOOP)
            with dve.Fori(DOWN_LOOP // 2, NM // 2) as j:
                for par in range(2):
                    down_unit(2 * j + par, par, NM + 1 + j, 0, 9)
            weight_lo(GU + NM - 1, wd[:, NM - 1, HI, :], wd[:, NM - 1, LO, :])
            for t in range(NT):
                dve.wait_ge(down_done, t + 1)
                v.scalar_tensor_tensor(res[:, t, :], bank[(t + 4) % 8][:], c_down, res[:, t, :],
                                       ALU.mult, ALU.add).then_inc(fin_done, 1)

        @block.tensor
        def _(pe):
            def transpose_tiles(c):
                for t in range(TPC * c, TPC * c + TPC):
                    pe.wait_ge(xn_done, t + 1)
                    if t >= 4:
                        pe.wait_ge(xlo_done, t - 3)
                    for f in range(NC):
                        mm = nc.tensor.transpose(bank[4 + t % 4][:, P * f:P * f + P],
                                                 xnb[:, t % 8, P * f:P * f + P], ident[:])
                    mm.then_inc(tp_done, 1)

            def products(k, par, c, pair, units=(0, 1)):
                for unit in units:
                    if c == 0:
                        pe.wait_ge(wlo_done, 2 * k + unit + 1)
                    out_b = bank[2 * pair + unit]
                    n = 0
                    for f in range(NC):
                        for wl, xl in ((HI, HI), (HI, LO), (LO, HI)):
                            mm = nc.tensor.matmul(out_b[:], w1[:, par, unit, wl, f, :],
                                                  xT[:, TPC * c:TPC * c + TPC, xl, f, :],
                                                  start=(n == 0), stop=(n == 3 * NC - 1))
                            n += 1
                    mm.then_inc((gate_done, up_done)[unit], 1)

            pe.wait_ge(id_done, 2)
            transpose_tiles(0)
            for c in range(NCH):
                if c >= 2:
                    pe.wait_ge(hlo_done, c - 1)
                pe.wait_ge(xlo_done, TPC * (c + 1))
                products(0, 0, c, c % 2, units=(0,))
                if c == 0:
                    pe.wait_ge(s4_ld, 48)
                    for i in range(2):
                        mm = nc.tensor.matmul(bank[3][:, i:i + 1], vcs[:, P * i:P * i + P], bps,
                                              start=True, stop=True)
                    mm.then_inc(b_mm, 1)
                if c + 1 < NCH:
                    transpose_tiles(c + 1)
                if c == 1:
                    pe.wait_ge(b_cp, 1)
                products(0, 0, c, c % 2, units=(1,))

            def window(k, par):
                for c in range(NCH):
                    if isinstance(k, int) and k == 1:
                        if c < 2:
                            pe.wait_ge(hlo_done, 3 + c)
                    else:
                        pe.wait_ge(hlo_done, NCH * k + c - 3)
                    if isinstance(k, int) and c == 3:
                        if k == NM - 4:
                            pe.wait_ge(s4_done, SUMS_READ)
                        elif k == NM - 2:
                            pe.wait_ge(t_done, 1)
                    products(k, par, c, c)
                    if isinstance(k, int) and c == 0:
                        if k == NM - 4:
                            s4_sums()
                        elif k == NM - 2:
                            toeplitz()

            def s4_sums():
                pe.wait_ge(hlo_done, NCH * (NM - 4))
                pe.wait_ge(v_done, V_STEPS)
                pe.wait_ge(inv_done, 2)
                for a in range(4):
                    rows = slice(64 * (a // 2), 64 * (a // 2) + 64)
                    f = P * (a % 2)
                    sums = bank[6 + a // 2][:, 8 * a:8 * a + 8]
                    nc.tensor.matmul(sums, e_re[rows, f:f + P], V[rows, 0, :],
                                     start=True, stop=False)
                    mm = nc.tensor.matmul(sums, e_im[rows, f:f + P], V[rows, 1, :],
                                          start=False, stop=True)
                mm.then_inc(sum_done, 1)

            def toeplitz():
                pe.wait_ge(u_done, 2)
                pe.wait_ge(hlo_done, NCH * (NM - 2))
                terms = (((0, 0), (3, 1)), ((2, 1), (3, 0)), ((2, 0), (1, 1)), ((0, 1), (1, 0)))
                for b in range(4):
                    n = 0
                    for a in range(4):
                        for u, cs in terms[a * b % 4]:
                            mm = nc.tensor.matmul(bank[6][:, P * b:P * b + P], U[u][:, a, :], rhs_t[:, cs, a, :],
                                                  start=(n == 0), stop=(n == 7))
                            n += 1
                mm.then_inc(toe_mm, 1)

            window(1, 1)
            with pe.Fori(2, NM - 5, 2) as k:
                window(k, 0)
                window(k + 1, 1)
            for k in range(NM - 4, NM):
                window(k, k % 2)

            pe.wait_ge(tz_done, 1)
            pe.wait_ge(hlo_done, NCH * NM - 2)
            for t in range(NT):
                if t >= 4:
                    pe.wait_ge(res_done, t - 3)
                n = 0
                for j in range(NC):
                    for xl, tl in ((HI, HI), (HI, LO), (LO, HI)):
                        mm = nc.tensor.matmul(bank[t % 4][:, P * j:HD], xT[:, t, xl, j, :],
                                              tz[:, tl, 0:HD - P * j], start=(n == 0), stop=(n == 3 * NC - 1))
                        n += 1
                mm.then_inc(conv_done, 1)

            def down(mt, t):
                if isinstance(mt, int) and mt == 0:
                    if t == 4:
                        pe.wait_ge(res_done, NT)
                    if t >= 8:
                        pe.wait_ge(fin_done, t - 7)
                for n, (hl, wl) in enumerate(((HI, HI), (HI, LO), (LO, HI))):
                    part = h[:, mt, hl, P * t:P * t + P]
                    if hl == LO:
                        part = part.bitcast(BF16)
                    mm = nc.tensor.matmul(bank[(t + 4) % 8][:], part, wd[:, mt, wl, :],
                                          start=(isinstance(mt, int) and mt == 0 and n == 0),
                                          stop=(isinstance(mt, int) and mt == NM - 1 and n == 2))
                if isinstance(mt, int) and mt == NM - 1:
                    mm.then_inc(down_done, 1)

            pe.wait_ge(hlo_done, NCH * NM)
            for group in range(2):
                tiles = range(8 * group, 8 * group + 8)
                pe.wait_ge(wlo_done, GU + 1)
                for t in tiles:
                    down(0, t)
                rest = NM - 1 if group == 0 else NM - 3
                with pe.Fori(1, rest) as mt:
                    pe.wait_ge(wlo_done, GU + 1 + mt)
                    for t in tiles:
                        down(mt, t)
                pe.wait_ge(wlo_done, GU + NM)
                for t in tiles:
                    for mt in range(rest, NM):
                        down(mt, t)


def _s4_tables(np):
    L = HD
    p, a, f = np.arange(P)[:, None, None], np.arange(4)[None, :, None], np.arange(P)[None, None, :]
    root = 4 * p + a
    rhs = 2 * np.pi * (root * f % L) / L
    lhs = np.pi * (root * (1 - 2 * f) % (2 * L)) / L
    rows = (4 * np.arange(P)[None, :] + np.arange(4)[:, None]).reshape(2, 256) * np.pi / L
    rows = np.repeat(rows, NST, axis=0)
    f32 = np.float32
    return (np.concatenate([np.cos(rows), np.sin(rows)], axis=1).astype(f32),
            np.stack([np.cos(rhs), np.sin(rhs)], axis=1).reshape(P, 2, 4, P).astype(f32),
            (np.stack([np.cos(lhs), np.sin(lhs)], axis=1) / L).reshape(P, 2, 4, P).astype(f32),
            np.cos(root[:, :, 0] * np.pi / L).astype(f32))


def kernel(**inputs):
    import numpy as np
    import concourse.bacc as bacc
    from concourse.bass_utils import run_bass_kernel_spmd

    i = {k: np.asarray(v) for k, v in inputs.items()}

    def gu_codes(q):
        return q.reshape(NM, P, NC, P).transpose(0, 3, 2, 1).reshape(NM, P, HD)

    def gu_absmax(am):
        return am.reshape(NM, P, NC, 2).transpose(0, 3, 2, 1).reshape(NM, 2, HD)

    vc = i["L0_attn_Vc_ri"].transpose(1, 2, 0)
    cols = np.concatenate([i["L0_attn_p_ri"], i["L0_attn_q_ri"], i["L0_attn_Ct_ri"].reshape(NST, 2),
                           i["L0_attn_Lambda_ri"]], axis=1)
    root_rows, tab_rhs, tab_lhs, cos_cols = _s4_tables(np)
    flat = np.stack([i["L0_ffn_gate_absmax"], i["L0_ffn_up_absmax"], i["L0_ffn_down_absmax"]])
    arrays = {
        "x": i["L0_attn_u"],
        "q_gate": gu_codes(i["L0_ffn_gate_q"]),
        "q_up": gu_codes(i["L0_ffn_up_q"]),
        "q_down": i["L0_ffn_down_q"].reshape(HD, NM, P).transpose(1, 2, 0),
        "am_gate": gu_absmax(i["L0_ffn_gate_absmax"]),
        "am_up": gu_absmax(i["L0_ffn_up_absmax"]),
        "am_down": i["L0_ffn_down_absmax"].reshape(HD, NM, 2).transpose(1, 2, 0),
        "am_flat": flat.reshape(3, P, HD * M // 64 // P),
        "s4_cols": np.concatenate([cols, cols], axis=0),
        "vct": np.concatenate([vc, vc], axis=2).reshape(NST, 2 * P),
        "bp": i["L0_attn_Bp"],
        "d_skip": i["L0_attn_D"].reshape(1, 1),
        "log_step": i["L0_attn_log_step"].reshape(1, 1),
        "lines_b": np.tile(np.array([b for _, b in NF4_LINES], np.float32), (P, 1)),
        "root_rows": root_rows,
        "tab_rhs": tab_rhs,
        "tab_lhs": tab_lhs,
        "cos_cols": cos_cols,
    }
    arrays = {f"in_{k}": np.ascontiguousarray(a) for k, a in arrays.items()}

    nc = bacc.Bacc("TRN2", target_bir_lowering=False, num_devices=1)
    args = [nc.dram_tensor(k, a.shape, mybir.dt.from_np(a.dtype), kind="ExternalInput").ap()
            for k, a in arrays.items()]
    args.append(nc.dram_tensor("out_0", i["L0_attn_u"].shape, F32, kind="ExternalOutput").ap())
    ffn_conv_kernel(nc, *args)
    r = run_bass_kernel_spmd(nc, [arrays], core_ids=[0])
    return r.results[0]["out_0"]
```

```python
import math
from contextlib import ExitStack

import concourse.bass as bass
from concourse import mybir

P = 128
F32 = mybir.dt.float32
F16 = mybir.dt.float16
BF16 = mybir.dt.bfloat16
I32 = mybir.dt.int32
ALU = mybir.AluOpType
ACT = mybir.ActivationFunctionType
AX = mybir.AxisListType

TOKENS, HD, M = 2048, 512, 1792
NT = TOKENS // P
NC = HD // P
NM = M // P
CH = 512
NCH = TOKENS // CH
TPC = CH // P
NST = 64
EPS = 1e-5

GU = 2 * NM
AHEAD = 10
BEHIND = 7
STEPS = 8
RING = 4
CONV_END = 42
DOWN_LOOP = 6
HI, LO = 0, 1

NF4_PIVOT = -0.025715956464409828
NF4_LINES = [
    (0.09119964390993118, -0.6639638543128967),
    (0.09966794401407242, -0.7088291049003601),
    (0.08134990185499191, -0.5455029606819153),
    (0.0918029397726059, -0.6462011337280273),
    (0.1301555633544922, -0.8111001253128052),
    (0.12190717458724976, -0.9964603185653687),
    (0.30380719900131226, -1.025715947151184),
    (0.2770431935787201, -3.129931926727295),
]

XS = 2.0 ** 11
EXP_BITS = 0x7F800000
RSQRT_MAGIC = 0x5F3759DF
ROUND_MAGIC = 1.5 * 2.0 ** 23
LN2_HI, LN2_LO = 0.693145751953125, 1.42860682030941723e-06
EXP_TERMS = 10


def ffn_conv_kernel(nc, x, q_gate, q_up, q_down, am_gate, am_up, am_down, am_flat, s4_cols, vct, bp,
                    d_skip, log_step, lines_b, root_rows, tab_rhs, tab_lhs, cos_cols, out):
    x_v = x.rearrange("b s d -> (b s) d").rearrange("(p t) d -> p t d", t=NT)
    out_v = out.rearrange("b s d -> (b s) d").rearrange("(p t) d -> p t d", t=NT)

    with ExitStack() as ctx:
        def sb(name, shape, dt):
            return ctx.enter_context(nc.sbuf_tensor(name, shape, dt))

        def sem(name):
            return ctx.enter_context(nc.semaphore(name))

        h = sb("h", [P, NM, 2, TOKENS], F16)
        xT = sb("xT", [P, NT, 2, NC, P], F16)
        wd = sb("wd", [P, NM, 2, HD], F16)
        w1 = sb("w1", [P, 2, 2, 2, NC, P], F16)
        line = sb("line", [P, RING, CH], F32)
        acc_l = sb("acc_l", [P, CH], F32)
        acc_r = sb("acc_r", [P, CH], F32)
        wt = sb("wt", [P, CH], F32)
        qs = sb("qs", [P, 2, CH], I32)
        am = sb("am", [P, 2, CH], F32)
        sil = sb("sil", [P, 2, CH], F32)
        ident = sb("ident", [P, P], F32)
        lb = sb("lb", [P, len(NF4_LINES)], F32)
        sc = sb("sc", [P, 28], F32)
        V = sb("V", [P, 2, 8], F32)
        V_halves = sb("V_halves", [P, 2, 16], F32)
        cols = sb("cols", [P, 8], F32)
        yv = sb("yv", [P, 16], F32)
        at_s = sb("at_s", [P, 68], F32)

        def borrow(tensor_rows, shape, dt=F32):
            flat = tensor_rows.rearrange("p a b c -> p (a b c)")
            if dt != F16:
                flat = flat.bitcast(dt)
            return flat[:, 0:shape]

        xs = borrow(h[:, NM - 4:NM], NT * HD).rearrange("p (t d) -> p t d", t=NT)
        xnb = borrow(h[:, NM - 6:NM - 4], 8 * HD).rearrange("p (t d) -> p t d", t=8)
        misc = borrow(h[:, NM - 7:NM - 6], 2048)
        st6 = misc[:, 0:6 * NT].rearrange("p (t s) -> p t s", t=NT)
        mv = misc[:, 128:128 + 2 * NT].rearrange("p (t s) -> p t s", t=NT)
        rs = misc[:, 192:192 + 6 * NT].rearrange("p (k t) -> p k t", k=6)
        amf = misc[:, 320:320 + 3 * 112].rearrange("p (k n) -> p k n", k=3)
        amx = misc[:, 704:710]
        vcs = misc[0:NST, 736:736 + 2 * P]
        bps = misc[0:NST, 1000:1001]
        lines_1 = borrow(h[:, 1:3], 8 * CH).rearrange("p (k n) -> p k n", k=8)
        s4b = wd[:, 5:NM].rearrange("p m a b -> p (m a b)").bitcast(F32).rearrange("p (k n) -> p k n", k=NM - 5)
        rhs_t = s4b[:, 0:2].rearrange("p k (a f) -> p k a f", a=4)
        lhs_t = s4b[:, 2:4].rearrange("p k (a f) -> p k a f", a=4)
        roots = s4b[:, 4]
        e_re, e_im = s4b[:, 5, 0:256], s4b[:, 5, 256:512]
        e_m1, e_m2 = s4b[:, 6, 0:256], s4b[:, 6, 256:512]
        U = [s4b[:, k].rearrange("p (a f) -> p a f", a=4) for k in (4, 5, 6, 7)]
        T = s4b[:, 4]
        tz = wd[:, NM - 1]
        xr = w1.rearrange("p a b c d e -> p (a b c d e)").bitcast(F32).rearrange("p (t d) -> p t d", t=4)
        res = xT.rearrange("p t a c f -> p (t a c f)").bitcast(F32).rearrange("p (t d) -> p t d", t=NT)

        amax, pow2, inv2 = sc[:, 0:3], sc[:, 3:6], sc[:, 6:9]
        s_w = [sc[:, 9 + s:10 + s] for s in range(3)]
        c_gate, c_up, c_down, c_conv = (sc[:, k:k + 1] for k in (12, 13, 14, 15))
        kmax, kpow, kinv, s_k = (sc[:, k:k + 1] for k in (16, 17, 18, 19))
        two_over_step, d_col, lstep, krow = (sc[:, k:k + 1] for k in (20, 21, 22, 23))

        def line_of(seq, k):
            return lines_1[:, k, :] if isinstance(seq, int) and seq == 1 else line[:, k % RING, :]

        e_int, e_rest, e_sum, e_pow = (sc[:, k:k + 1] for k in (24, 25, 26, 27))

        bank = [ctx.enter_context(nc.psum_tensor(f"bank{b}", [P, CH], F32)) for b in range(8)]

        q_ld = [sem(f"q_ld{b}") for b in range(2)]
        am_ld = [sem(f"am_ld{b}") for b in range(2)]
        x0_ld = [sem(f"x0_ld{i}") for i in range(TPC // 2)]
        x_ld = [sem(f"x_ld{c}") for c in range(1, NCH)]
        lb_ld = sem("lb_ld")
        step_ld = sem("step_ld")
        d_ld = sem("d_ld")
        amf_ld = sem("amf_ld")
        s4_ld = sem("s4_ld")
        tab_ld = sem("tab_ld")
        xr_ld = [sem(f"xr_ld{b}") for b in range(4)]
        out_st = sem("out_st")
        id_done = sem("id_done")
        line_done = sem("line_done")
        dq_done = sem("dq_done")
        whi_done = sem("whi_done")
        wlo_done = sem("wlo_done")
        sc_done = sem("sc_done")
        mx_done = sem("mx_done")
        st_done = sem("st_done")
        mv_done = sem("mv_done")
        rs_step = sem("rs_step")
        xn_done = sem("xn_done")
        tp_done = sem("tp_done")
        xhi_done = sem("xhi_done")
        xlo_done = sem("xlo_done")
        gate_done = sem("gate_done")
        up_done = sem("up_done")
        silu_done = sem("silu_done")
        h_done = sem("h_done")
        hhi_done = sem("hhi_done")
        hlo_done = sem("hlo_done")
        step_done = sem("step_done")
        b_mm = sem("b_mm")
        b_cp = sem("b_cp")
        v_done = sem("v_done")
        s4_done = sem("s4_done")
        inv_done = sem("inv_done")
        u_done = sem("u_done")
        t_done = sem("t_done")
        kmax_done = sem("kmax_done")
        tz_done = sem("tz_done")
        sum_done = sem("sum_done")
        toe_mm = sem("toe_mm")
        tri_done = sem("tri_done")
        conv_done = sem("conv_done")
        res_done = sem("res_done")
        down_done = sem("down_done")
        fin_done = sem("fin_done")

        RSTD = 18
        EXP_STEPS = 7 + EXP_TERMS
        SUMS_READ = 8
        V_STEPS = 20
        block = ctx.enter_context(nc.Block())

        @block.sync
        def _(sp):
            def load_absmax(slot, am_src):
                for s in range(2):
                    sp.dma_start(am[64 * s:64 * s + 64, slot, :],
                                 am_src[s:s + 1, :].to_broadcast([64, CH])).then_inc(am_ld[slot], 16)

            def load_unit(seq, slot, q_src, am_src, wait):
                if wait:
                    sp.wait_ge(line_done, 8 * (seq - 1))
                sp.dma_start(qs[:, slot, :], q_src).then_inc(q_ld[slot], 16)
                if wait:
                    sp.wait_ge(dq_done, STEPS * (seq - 1))
                load_absmax(slot, am_src)

            def load_gu(mt, wait=True):
                load_unit(2 * mt, 0, q_gate[mt], am_gate[mt], wait)
                load_unit(2 * mt + 1, 1, q_up[mt], am_up[mt], wait)

            sp.dma_start(lb[:], lines_b).then_inc(lb_ld, 16)
            sp.dma_start(qs[:, 0, :], q_gate[0]).then_inc(q_ld[0], 16)
            sp.dma_start(xs[:, 0:2, :], x_v[:, 0:2, :]).then_inc(x0_ld[0], 16)
            sp.dma_start(amf, am_flat).then_inc(amf_ld, 16)
            sp.dma_start(xs[:, 2:4, :], x_v[:, 2:4, :]).then_inc(x0_ld[1], 16)
            sp.dma_start(lstep, log_step.to_broadcast([P, 1])).then_inc(step_ld, 16)
            sp.dma_start(qs[:, 1, :], q_up[0]).then_inc(q_ld[1], 16)
            load_absmax(0, am_gate[0])
            load_absmax(1, am_up[0])
            sp.dma_start(d_col, d_skip.to_broadcast([P, 1])).then_inc(d_ld, 16)
            for c in range(1, NCH):
                sp.dma_start(xs[:, TPC * c:TPC * c + TPC, :],
                             x_v[:, TPC * c:TPC * c + TPC, :]).then_inc(x_ld[c - 1], 16)
                if c == 1:
                    sp.dma_start(cols[:], s4_cols).then_inc(s4_ld, 16)
                    sp.dma_start(vcs, vct).then_inc(s4_ld, 16)
                    sp.dma_start(bps, bp).then_inc(s4_ld, 16)
            load_gu(1)
            sp.dma_start(rhs_t, tab_rhs).then_inc(tab_ld, 16)
            sp.dma_start(lhs_t, tab_lhs).then_inc(tab_ld, 16)
            sp.dma_start(roots, root_rows).then_inc(tab_ld, 16)
            sp.dma_start(at_s[:, 32:36], cos_cols).then_inc(tab_ld, 16)
            with sp.Fori(2, NM) as mt:
                load_gu(mt)
            def load_down(mt, par):
                load_unit(GU + mt, par, q_down[mt], am_down[mt], True)

            for mt in range(4):
                load_down(mt, mt % 2)
            for t in range(NT):
                if t < 4:
                    sp.wait_ge(up_done, NCH * (NM - 1 + t // 2))
                else:
                    sp.wait_ge(res_done, t - 3)
                sp.dma_start(xr[:, t % 4, :], x_v[:, t, :]).then_inc(xr_ld[t % 4], 16)
                if t in (3, 12):
                    load_down(4 + t // 12, t // 12)
            with sp.Fori(DOWN_LOOP, NM - 1, 2) as mt:
                for par in range(2):
                    load_down(mt + par, par)
            for t in range(NT):
                sp.wait_ge(fin_done, t + 1)
                sp.dma_start(out_v[:, t, :], res[:, t, :]).then_inc(out_st, 16)
            sp.wait_ge(out_st, 16 * NT)

        @block.gpsimd
        def _(pool):
            pool.memset(ident[:], 0.0).then_inc(id_done, 1)
            pool.wait_ge(id_done, 1)
            pool.affine_select(out=ident[:], in_=ident[:], compare_op=ALU.not_equal, fill=1.0, base=0,
                               pattern=[[-1, P]], channel_multiplier=1).then_inc(id_done, 1)
            pool.wait_ge(sc_done, 1)
            pool.partition_all_reduce(amax, amx[:, 0:3], P, bass.bass_isa.ReduceOp.max).then_inc(mx_done, 1)

            rs_n = [0]

            def rs_next(op, *args, wait=True):
                if wait:
                    pool.wait_ge(rs_step, rs_n[0])
                op(*args).then_inc(rs_step, 1)
                rs_n[0] += 1

            for c in range(NCH):
                a, b = TPC * c, TPC * c + TPC
                v, hv, y, t = (rs[:, i, a:b] for i in range(4))
                pool.wait_ge(mv_done, b)
                rs_next(pool.tensor_scalar, v, mv[:, a:b, 1], EPS, None, ALU.add, wait=False)
                rs_next(pool.tensor_scalar, hv, mv[:, a:b, 1], EPS, -0.5, ALU.add, ALU.mult, wait=False)
                rs_next(pool.tensor_scalar, y.bitcast(I32), v.bitcast(I32), -0.5, float(RSQRT_MAGIC),
                        ALU.mult, ALU.add)
                for _ in range(3):
                    rs_next(pool.tensor_tensor, t, y, y, ALU.mult)
                    rs_next(pool.tensor_tensor, t, t, hv, ALU.mult)
                    rs_next(pool.tensor_scalar, t, t, 1.5, None, ALU.add)
                    rs_next(pool.tensor_tensor, y, y, t, ALU.mult)
                rs_next(pool.tensor_scalar, t, y, -XS, None, ALU.mult)
                rs_next(pool.tensor_scalar, rs[:, 4, a:b], y, XS, None, ALU.mult, wait=False)
                rs_next(pool.tensor_tensor, rs[:, 5, a:b], mv[:, a:b, 0], t, ALU.mult)

            pool.wait_ge(step_ld, 16)
            step_n = [0]

            def exp_next(op, *args):
                pool.wait_ge(step_done, step_n[0])
                op(*args).then_inc(step_done, 1)
                step_n[0] += 1

            pool.tensor_scalar(e_int, lstep, -1.0 / math.log(2.0), ROUND_MAGIC,
                               ALU.mult, ALU.add).then_inc(step_done, 1)
            step_n[0] += 1
            exp_next(pool.tensor_scalar, e_int, e_int, -ROUND_MAGIC, None, ALU.add)
            exp_next(pool.tensor_scalar, e_rest, e_int, LN2_HI, lstep, ALU.mult, ALU.add)
            exp_next(pool.tensor_scalar, e_sum, e_int, LN2_LO, e_rest, ALU.mult, ALU.add)
            exp_next(pool.tensor_copy, e_rest, e_sum)
            series = [(-1.0) ** k / math.factorial(k) for k in range(EXP_TERMS + 1)]
            exp_next(pool.tensor_scalar, e_sum, e_rest, series[EXP_TERMS], series[EXP_TERMS - 1], ALU.mult, ALU.add)
            for k in range(EXP_TERMS - 2, -1, -1):
                exp_next(pool.tensor_scalar, e_sum, e_sum, e_rest, series[k], ALU.mult, ALU.add)
            exp_next(pool.tensor_scalar, e_pow.bitcast(I32), e_int, 128.0, 2.0 ** 23, ALU.add, ALU.mult)
            exp_next(pool.tensor_tensor, two_over_step, e_sum, e_pow, ALU.mult)

            pool.wait_ge(s4_ld, 48)
            pool.wait_ge(b_cp, 1)

            def chained(ins):
                ins.then_inc(v_done, 1)

            chained(pool.memset(V_halves[:], 0.0))
            chained(pool.tensor_copy(yv[:, 4:6], cols[:, 0:2]))
            chained(pool.tensor_copy(yv[:, 2:3], yv[:, 1:2]))
            chained(pool.tensor_scalar(yv[:, 3:4], yv[:, 0:1], -1.0, None, ALU.mult))
            chained(pool.tensor_copy(yv[:, 6:7], cols[:, 1:2]))
            chained(pool.tensor_scalar(yv[:, 7:8], cols[:, 0:1], -1.0, None, ALU.mult))
            pool.wait_ge(v_done, 6)
            for i, a in enumerate((4, 2)):
                for j in range(2):
                    k = 2 * i + j
                    chained(pool.tensor_scalar(V[:, 0, 2 * k:2 * k + 2], yv[:, 4 * j:4 * j + 2],
                                               cols[:, a:a + 1], None, ALU.mult))
                    chained(pool.tensor_scalar(yv[:, 8 + 2 * k:10 + 2 * k], yv[:, 4 * j + 2:4 * j + 4],
                                               cols[:, a + 1:a + 2], None, ALU.mult))
            pool.wait_ge(v_done, 14)
            chained(pool.tensor_tensor(V[:, 0, :], V[:, 0, :], yv[:, 8:16], ALU.add))
            pool.wait_ge(v_done, 15)
            v0 = V[:, 0, :].rearrange("p (k c) -> p k c", c=2)
            v1 = V[:, 1, :].rearrange("p (k c) -> p k c", c=2)
            chained(pool.tensor_copy(v1[:, :, 0], v0[:, :, 1]))
            chained(pool.tensor_scalar(v1[:, :, 1], v0[:, :, 0], -1.0, None, ALU.mult))
            pool.wait_ge(v_done, 17)
            chained(pool.tensor_scalar(V[:, 0, :], V[:, 0, :], -1.0, None, ALU.mult))
            pool.wait_ge(v_done, 18)
            for half in range(2):
                rows = slice(NST * half, NST * half + NST)
                chained(pool.tensor_copy(V_halves[rows, :, 8 * half:8 * half + 8], V[rows]))
            pool.wait_ge(t_done, 3)
            pool.affine_select(out=T[:, 0:P], in_=T[:, 0:P], compare_op=ALU.is_ge, fill=0.0, base=0,
                               pattern=[[1, P]], channel_multiplier=-1).then_inc(tri_done, 1)
            pool.wait_ge(t_done, 4)
            pool.partition_all_reduce(kmax, krow, P, bass.bass_isa.ReduceOp.max).then_inc(kmax_done, 1)

        @block.scalar
        def _(act):
            def make_line(seq, slot, loads, k):
                if k == 0:
                    act.wait_ge(q_ld[slot], 16 * loads)
                if isinstance(seq, int) and seq == 2 and k < RING:
                    act.wait_ge(dq_done, 3 + k)
                elif not (isinstance(seq, int) and (seq == 1 or seq == 0 and k < RING)):
                    act.wait_ge(dq_done, STEPS * (seq - 1) + 3 + k if k < RING else STEPS * seq + (k - 2) // 2)
                slope = NF4_LINES[k][0]
                nc.scalar.activation(line_of(seq, k), qs[:, slot, :], ACT.Identity, scale=slope,
                                     bias=lb[:, k:k + 1]).then_inc(line_done, 1)

            def weight_hi(seq, dst, free=None):
                act.wait_ge(dq_done, STEPS * (seq + 1))
                if free is not None:
                    act.wait_ge(up_done, free)
                nc.scalar.activation(dst, wt[:], ACT.Copy).then_inc(whi_done, 1)

            def items(mt, par, first, last):
                for p in range(first, last):
                    unit, i = p // 9, p % 9
                    if i != 4:
                        make_line(2 * mt + unit, unit % 2, mt + 1 + unit // 2, i if i < 4 else i - 1)
                        continue
                    before, buf = mt + (unit - 1) // 2, (par + (unit - 1) // 2) % 2
                    free = None if isinstance(before, int) and before < 2 else NCH * (before - 1)
                    which = (unit - 1) % 2
                    weight_hi(2 * mt + unit - 1, w1[:, buf, which, HI].rearrange("p c f -> p (c f)"), free)

            def down_unit(mt, slot, loads, first, last):
                for i in range(first, last):
                    if i != 4:
                        make_line(GU + mt, slot, loads, i if i < 4 else i - 1)
                    else:
                        weight_hi(GU + mt - 1, wd[:, mt - 1, HI, :])

            def down_items(first, last):
                for p in range(first, last):
                    mt = p // 9
                    down_unit(mt, mt % 2, NM + 1 + mt // 2, p % 9, p % 9 + 1)

            def silu(k, c, pair):
                n = NCH * k + c
                act.wait_ge(gate_done, n + 1)
                if not (isinstance(k, int) and n < 2):
                    act.wait_ge(h_done, n - 1)
                nc.scalar.activation(sil[:, c % 2, :], bank[2 * pair][:], ACT.Silu,
                                     scale=c_gate).then_inc(silu_done, 1)

            def h_hi(k, c, pair):
                n = NCH * k + c
                act.wait_ge(h_done, n + 1)
                nc.scalar.activation(h[:, k, HI, CH * c:CH * c + CH], bank[2 * pair + 1][:],
                                     ACT.Copy).then_inc(hhi_done, 1)

            def norm(t):
                act.wait_ge(rs_step, RSTD * (t // TPC + 1))
                if t >= 8:
                    act.wait_ge(tp_done, t - 7)
                nc.scalar.activation(xnb[:, t % 8, :], xs[:, t, :], ACT.Identity, scale=rs[:, 4, t:t + 1],
                                     bias=rs[:, 5, t:t + 1]).then_inc(xn_done, 1)

            def x_hi(t):
                act.wait_ge(tp_done, t + 1)
                nc.scalar.activation(xT[:, t, HI].rearrange("p c f -> p (c f)"), bank[4 + t % 4][:],
                                     ACT.Copy).then_inc(xhi_done, 1)

            def window(k, par):
                for c in range(NCH):
                    silu(k, c, c)
                    items(k + 1, 1 - par, AHEAD + 18 * 2 * c // 8, AHEAD + 18 * (2 * c + 1) // 8)
                    h_hi(k, c, c)
                    items(k + 1, 1 - par, AHEAD + 18 * (2 * c + 1) // 8, AHEAD + 18 * (2 * c + 2) // 8)

            act.wait_ge(lb_ld, 16)
            nc.scalar.activation(sil[:, 0, 0:1], lb[:, 0:1], ACT.Silu)
            items(0, 0, 0, 4)
            items(0, 0, 5, 9)
            items(0, 0, 9, 13)
            items(0, 0, 14, 18)
            items(0, 0, 13, 14)
            norm(0)
            for t in range(1, 4):
                norm(t)
                x_hi(t - 1)
            x_hi(3)
            norm(4)
            for t in range(5, 8):
                norm(t)
                x_hi(t - 1)
            x_hi(7)
            items(0, 0, 18, 24)
            silu(0, 0, 0)
            for t in range(8, 12):
                norm(t)
            items(0, 0, 24, 26)
            silu(0, 1, 1)
            act.wait_ge(b_mm, 1)
            nc.scalar.activation(yv[:, 0:2], bank[3][:, 0:2], ACT.Copy).then_inc(b_cp, 1)
            for t in range(8, 12):
                x_hi(t)
            items(0, 0, 26, 27)
            for t in range(12, 16):
                norm(t)
            h_hi(0, 0, 0)
            items(0, 0, 27, 30)
            h_hi(0, 1, 1)
            for t in range(12, 16):
                x_hi(t)
            items(0, 0, 30, 34)
            silu(0, 2, 0)
            items(0, 0, 34, 37)
            h_hi(0, 2, 0)
            items(0, 0, 37, 40)
            silu(0, 3, 1)
            items(0, 0, 40, 44)
            h_hi(0, 3, 1)
            items(0, 0, 44, 36 + AHEAD)
            with act.Fori(1, NM - 2, 2) as k:
                window(k, 1)
                window(k + 1, 0)
            for c in range(NCH):
                silu(NM - 1, c, c)
                down_items(AHEAD + 18 * 2 * c // 8, AHEAD + 18 * (2 * c + 1) // 8)
                h_hi(NM - 1, c, c)
                down_items(AHEAD + 18 * (2 * c + 1) // 8, AHEAD + 18 * (2 * c + 2) // 8)
            down_items(18 + AHEAD, 9 * DOWN_LOOP)
            with act.Fori(DOWN_LOOP // 2, NM // 2) as j:
                for par in range(2):
                    down_unit(2 * j + par, par, NM + 1 + j, 0, 9)
            act.wait_ge(conv_done, NT)
            weight_hi(GU + NM - 1, wd[:, NM - 1, HI, :])

        @block.vector
        def _(dve):
            def step(seq, slot, loads, s_scale, s):
                made = 8 * seq
                if s == 0:
                    dve.wait_ge(line_done, made + 2)
                    ins = nc.vector.scalar_tensor_tensor(acc_l[:], line_of(seq, 0), NF4_PIVOT, line_of(seq, 1),
                                                         ALU.min, ALU.min)
                elif s == 1:
                    dve.wait_ge(line_done, made + 4)
                    ins = nc.vector.tensor_tensor(acc_r[:], line_of(seq, 2), line_of(seq, 3), ALU.max)
                elif s < 6:
                    dve.wait_ge(line_done, made + 3 + s)
                    dve.wait_ge(dq_done, STEPS * seq + s - 1)
                    acc, op = ((acc_l, ALU.min), (acc_r, ALU.max))[s % 2]
                    ins = nc.vector.tensor_tensor(acc[:], acc[:], line_of(seq, 2 + s), op)
                elif s == 6:
                    dve.wait_ge(dq_done, STEPS * seq + 6)
                    ins = nc.vector.scalar_tensor_tensor(wt[:], acc_r[:], -NF4_PIVOT, acc_l[:],
                                                         ALU.max, ALU.add)
                else:
                    dve.wait_ge(am_ld[slot], 32 * loads)
                    dve.wait_ge(dq_done, STEPS * seq + 7)
                    ins = nc.vector.scalar_tensor_tensor(wt[:], wt[:], s_w[s_scale], am[:, slot, :],
                                                         ALU.mult, ALU.mult)
                ins.then_inc(dq_done, 1)

            def weight_lo(seq, hi, lo):
                dve.wait_ge(whi_done, seq + 1)
                nc.vector.tensor_tensor(lo, wt[:], hi, ALU.subtract).then_inc(wlo_done, 1)

            def items(mt, par, first, last):
                for p in range(first, last):
                    unit, i = p // 9, p % 9
                    if i != 2:
                        step(2 * mt + unit, unit % 2, mt + 1 + unit // 2, unit % 2, i if i < 2 else i - 1)
                        continue
                    buf = (par + (unit - 1) // 2) % 2
                    w = w1[:, buf, (unit - 1) % 2].rearrange("p l c f -> p l (c f)")
                    weight_lo(2 * mt + unit - 1, w[:, HI, :], w[:, LO, :])

            def down_unit(mt, slot, loads, first, last):
                for i in range(first, last):
                    if i != 2:
                        step(GU + mt, slot, loads, 2, i if i < 2 else i - 1)
                    else:
                        weight_lo(GU + mt - 1, wd[:, mt - 1, HI, :], wd[:, mt - 1, LO, :])

            def down_items(first, last):
                for p in range(first, last):
                    mt = p // 9
                    down_unit(mt, mt % 2, NM + 1 + mt // 2, p % 9, p % 9 + 1)

            def h_mul(k, c, pair):
                n = NCH * k + c
                dve.wait_ge(up_done, n + 1)
                dve.wait_ge(silu_done, n + 1)
                up = bank[2 * pair + 1]
                nc.vector.scalar_tensor_tensor(up[:], up[:], c_up, sil[:, c % 2, :],
                                               ALU.mult, ALU.mult).then_inc(h_done, 1)

            def h_lo(k, c, pair):
                n = NCH * k + c
                dve.wait_ge(hhi_done, n + 1)
                nc.vector.tensor_tensor(h[:, k, LO, CH * c:CH * c + CH].bitcast(BF16), bank[2 * pair + 1][:],
                                        h[:, k, HI, CH * c:CH * c + CH], ALU.subtract).then_inc(hlo_done, 1)

            sc_n = [0]

            def small(op, *args, **kw):
                dve.wait_ge(sc_done, sc_n[0])
                op(*args, **kw).then_inc(sc_done, 1)
                sc_n[0] += 1

            def exponent(s, maxima, power, inverse):
                if s == 0:
                    small(nc.vector.tensor_scalar, maxima, maxima, 2.0 ** -40, None, ALU.max)
                elif s == 1:
                    small(nc.vector.tensor_scalar, power.bitcast(I32), maxima.bitcast(I32), EXP_BITS, None,
                          ALU.bitwise_and)
                else:
                    small(nc.vector.tensor_scalar, inverse.bitcast(I32), power.bitcast(I32), EXP_BITS, None,
                          ALU.bitwise_xor)

            SCALES = 8

            def scales(s):
                if s == 0:
                    dve.wait_ge(mx_done, 1)
                if s < 3:
                    exponent(s, amax, pow2, inv2)
                elif s == 3:
                    small(nc.vector.tensor_scalar, sc[:, 9:12], inv2, 2.0 ** 13, None, ALU.mult)
                elif s == 4:
                    small(nc.vector.tensor_scalar, c_gate, pow2[:, 0:1], 2.0 ** -14 / XS, None, ALU.mult)
                elif s == 5:
                    small(nc.vector.tensor_scalar, c_up, inv2[:, 0:1], 2.0 ** -6 * 2.0 ** -14 / XS, None, ALU.mult)
                elif s == 6:
                    small(nc.vector.tensor_scalar, c_down, pow2[:, 0:1], pow2[:, 1:2], 2.0 ** -9, ALU.mult, ALU.mult)
                else:
                    small(nc.vector.tensor_scalar, c_down, c_down, pow2[:, 2:3], None, ALU.mult)

            def stats(t):
                if t < TPC:
                    dve.wait_ge(x0_ld[t // 2], 16)
                else:
                    dve.wait_ge(x_ld[t // TPC - 1], 16)
                nc.vector.bn_stats(st6[:, t, :], xs[:, t, :]).then_inc(st_done, 1)

            def moments(c):
                for t in range(TPC * c, TPC * c + TPC):
                    dve.wait_ge(st_done, t + 1)
                    nc.vector.bn_aggr(mv[:, t, :], st6[:, t, :]).then_inc(mv_done, 1)

            def x_lo(t):
                dve.wait_ge(xhi_done, t + 1)
                hi, lo = (xT[:, t, i].rearrange("p c f -> p (c f)") for i in (HI, LO))
                nc.vector.tensor_tensor(lo, bank[4 + t % 4][:], hi, ALU.subtract).then_inc(xlo_done, 1)

            items(0, 0, 0, 1)
            stats(0)
            dve.wait_ge(amf_ld, 16)
            nc.vector.tensor_reduce(amx[:, 0:3], amf, AX.X, ALU.max,
                                    apply_absolute_value=True).then_inc(sc_done, 1)
            sc_n[0] = 1
            stats(1)
            items(0, 0, 1, 2)
            scales(0)
            stats(2)
            scales(1)
            stats(3)
            scales(2)
            moments(0)
            for i in range(3, SCALES):
                scales(i)
                items(0, 0, i, i + 1)
            dve.wait_ge(sc_done, 1 + SCALES)
            items(0, 0, SCALES, 9)
            for t in range(4, 8):
                stats(t)
            moments(1)
            items(0, 0, 9, 14)
            for t in range(0, 4):
                x_lo(t)
                stats(8 + t)
            moments(2)
            items(0, 0, 14, 16)
            for t in range(4, 8):
                x_lo(t)
                items(0, 0, 12 + t, 13 + t)
            for t in range(12, 16):
                stats(t)
            moments(3)
            items(0, 0, 20, 23)
            x_lo(8)
            x_lo(9)
            items(0, 0, 23, 24)
            x_lo(10)
            items(0, 0, 24, 25)
            x_lo(11)
            h_mul(0, 0, 0)
            items(0, 0, 25, 27)
            h_lo(0, 0, 0)
            h_mul(0, 1, 1)
            items(0, 0, 27, 28)
            x_lo(12)
            h_lo(0, 1, 1)
            x_lo(13)
            items(0, 0, 28, 30)
            x_lo(14)
            x_lo(15)
            items(0, 0, 30, 32)
            h_mul(0, 2, 0)
            items(0, 0, 32, 34)
            h_lo(0, 2, 0)
            items(0, 0, 34, 39)
            h_mul(0, 3, 1)
            items(0, 0, 39, 41)
            h_lo(0, 3, 1)
            items(0, 0, 41, 36 + BEHIND)

            def window(k, par, stage=None):
                for c in range(NCH):
                    h_mul(k, c, c)
                    items(k + 1, 1 - par, BEHIND + 18 * 2 * c // 8, BEHIND + 18 * (2 * c + 1) // 8)
                    if stage:
                        stage(2 * c)
                    h_lo(k, c, c)
                    items(k + 1, 1 - par, BEHIND + 18 * (2 * c + 1) // 8, BEHIND + 18 * (2 * c + 2) // 8)
                    if stage:
                        stage(2 * c + 1)

            with dve.Fori(1, NM - 8, 2) as k:
                window(k, 1)
                window(k + 1, 0)

            v = nc.vector
            s4_n, s4_wait = [0], [False]

            def s4(op, *args, more=False, done=s4_done):
                if s4_wait[0]:
                    dve.wait_ge(s4_done, s4_n[0])
                op(*args).then_inc(done, 1)
                s4_n[0] += done is s4_done
                s4_wait[0] = not more

            def inverse_e(s):
                if s == 0:
                    dve.wait_ge(tab_ld, 64)
                    dve.wait_ge(s4_ld, 48)
                    dve.wait_ge(step_done, EXP_STEPS)
                    s4(v.tensor_scalar, e_m1, roots[:, 0:256], cols[:, 7:8], None, ALU.mult)
                elif s == 1:
                    s4(v.scalar_tensor_tensor, e_im, roots[:, 256:512], two_over_step, e_m1,
                       ALU.mult, ALU.subtract, more=True)
                elif s == 2:
                    s4(v.tensor_scalar, e_re, roots[:, 0:256], cols[:, 6:7], None, ALU.mult)
                    s4(v.tensor_tensor, e_m1, e_re, e_re, ALU.mult, more=True)
                elif s == 3:
                    s4(v.tensor_tensor, e_m2, e_im, e_im, ALU.mult)
                    s4(v.tensor_tensor, e_m1, e_m1, e_m2, ALU.add)
                elif s == 4:
                    s4(v.reciprocal, e_m2, e_m1)
                elif s == 5:
                    s4(v.tensor_tensor, e_re, e_re, e_m2, ALU.mult, more=True, done=inv_done)
                    s4(v.tensor_tensor, e_im, e_im, e_m2, ALU.mult, more=True, done=inv_done)

            S = at_s[:, 0:32].rearrange("p (a k) -> p a k", a=4)
            cos_l = at_s[:, 32:36]
            s00, s01, s10, s11 = ((S[:, :, 2 * k], S[:, :, 2 * k + 1]) for k in range(4))
            nr, ni, dr, di, t0, t1, t2, t3 = (at_s[:, 36 + 4 * i:40 + 4 * i] for i in range(8))

            def at_roots(s):
                if s == 0:
                    dve.wait_ge(sum_done, 1)
                    s4(v.tensor_copy, at_s[:, 0:32].rearrange("p (h f k) -> p h f k", h=2, f=2),
                       bank[6][:, 0:32].rearrange("p (f h k) -> p h f k", f=2, h=2))
                elif s == 1:
                    s4(v.tensor_tensor, nr, s01[0], s10[0], ALU.mult, more=True)
                    s4(v.tensor_tensor, t0, s01[1], s10[1], ALU.mult, more=True)
                    s4(v.tensor_tensor, ni, s01[0], s10[1], ALU.mult, more=True)
                    s4(v.tensor_tensor, t1, s01[1], s10[0], ALU.mult, more=True)
                    s4(v.tensor_tensor, dr, cos_l, s11[0], ALU.mult, more=True)
                    s4(v.tensor_tensor, di, cos_l, s11[1], ALU.mult)
                    s4(v.tensor_tensor, nr, nr, t0, ALU.subtract, more=True)
                    s4(v.tensor_tensor, ni, ni, t1, ALU.add, more=True)
                elif s == 2:
                    s4(v.tensor_scalar, dr, dr, 1.0, None, ALU.add)
                    s4(v.tensor_tensor, t0, dr, dr, ALU.mult, more=True)
                    s4(v.tensor_tensor, t1, di, di, ALU.mult)
                    s4(v.tensor_tensor, t0, t0, t1, ALU.add)
                elif s == 3:
                    s4(v.reciprocal, t1, t0)
                    s4(v.tensor_tensor, t2, t1, cos_l, ALU.mult)
                    s4(v.tensor_tensor, nr, nr, t2, ALU.mult, more=True)
                    s4(v.tensor_tensor, ni, ni, t2, ALU.mult)
                else:
                    s4(v.tensor_tensor, t0, nr, dr, ALU.mult, more=True)
                    s4(v.tensor_tensor, t1, ni, di, ALU.mult)
                    s4(v.tensor_tensor, t0, t0, t1, ALU.add, more=True)
                    s4(v.tensor_tensor, t3, ni, dr, ALU.mult, more=True)
                    s4(v.tensor_tensor, t2, nr, di, ALU.mult)
                    s4(v.tensor_tensor, t1, t3, t2, ALU.subtract)
                    s4(v.tensor_tensor, nr, s00[0], t0, ALU.subtract, more=True)
                    s4(v.tensor_tensor, ni, s00[1], t1, ALU.subtract)

            def u_rows(s):
                if s < 2:
                    for a in range(2 * s, 2 * s + 2):
                        s4(v.tensor_scalar, U[2][:, a, :], lhs_t[:, 1, a, :], ni[:, a:a + 1], None, ALU.mult,
                           more=True)
                        s4(v.tensor_scalar, U[3][:, a, :], lhs_t[:, 1, a, :], nr[:, a:a + 1], None, ALU.mult,
                           more=(a < 3))
                elif s == 2:
                    for a in range(4):
                        s4(v.scalar_tensor_tensor, U[0][:, a, :], lhs_t[:, 0, a, :], nr[:, a:a + 1],
                           U[2][:, a, :], ALU.mult, ALU.subtract, more=True)
                        s4(v.scalar_tensor_tensor, U[1][:, a, :], lhs_t[:, 0, a, :], ni[:, a:a + 1],
                           U[3][:, a, :], ALU.mult, ALU.add, more=(a < 3))
                else:
                    s4(v.tensor_scalar, s4b[:, 6], s4b[:, 4], -1.0, None, ALU.mult, more=True, done=u_done)
                    s4(v.tensor_scalar, s4b[:, 7], s4b[:, 5], -1.0, None, ALU.mult, more=True, done=u_done)

            def toeplitz(s):
                if s == 0:
                    dve.wait_ge(toe_mm, 1)
                    even, odd = (bank[6][:].rearrange("p (i j f) -> p i j f", i=2, j=2)[:, :, j] for j in range(2))
                    T_b = T.rearrange("p (h i f) -> p h i f", h=2, i=2)
                    v.tensor_copy(T_b[:, 0], even).then_inc(t_done, 1)
                    dve.wait_ge(t_done, 1)
                    v.tensor_tensor(T_b[:, 1], T_b[:, 0], odd, ALU.subtract).then_inc(t_done, 1)
                    v.tensor_tensor(T_b[:, 0], T_b[:, 0], odd, ALU.add).then_inc(t_done, 1)
                elif s == 1:
                    dve.wait_ge(tri_done, 1)
                    dve.wait_ge(d_ld, 16)
                    s4(v.scalar_tensor_tensor, T[:, 0:P], ident[:], d_col, T[:, 0:P], ALU.mult, ALU.add)
                elif s == 2:
                    dve.wait_ge(s4_done, s4_n[0])
                    v.tensor_reduce(krow, T, AX.X, ALU.max, apply_absolute_value=True).then_inc(t_done, 1)
                elif s == 3:
                    dve.wait_ge(kmax_done, 1)
                    for i in range(3):
                        exponent(i, kmax, kpow, kinv)
                    small(v.tensor_scalar, s_k, kinv, 2.0 ** 13, None, ALU.mult)
                    small(v.tensor_scalar, c_conv, kpow, 2.0 ** -14 / XS, None, ALU.mult)
                else:
                    dve.wait_ge(sc_done, sc_n[0])
                    s4(v.tensor_scalar, tz[:, HI, :], T, s_k, None, ALU.mult)
                    s4(v.scalar_tensor_tensor, tz[:, LO, :], T, s_k, tz[:, HI, :], ALU.mult, ALU.subtract,
                       done=tz_done)

            def inverse_stage(slot):
                if slot % 2 == 1 and slot < 6:
                    inverse_e(slot // 2)

            def inverse_stage_2(slot):
                if slot % 2 == 1 and slot < 6:
                    inverse_e(3 + slot // 2)

            def roots_stage(slot):
                if 2 <= slot < 7:
                    at_roots(slot - 2)

            def rows_stage(slot):
                if slot % 2 == 0:
                    u_rows(slot // 2)

            def toeplitz_stage(slot):
                if 2 <= slot < 7:
                    toeplitz(slot - 2)

            window(NM - 7, 1, stage=inverse_stage)
            window(NM - 6, 0, stage=inverse_stage_2)
            window(NM - 5, 1)
            window(NM - 4, 0, stage=roots_stage)
            window(NM - 3, 1, stage=rows_stage)
            window(NM - 2, 0, stage=toeplitz_stage)
            for c in range(NCH):
                h_mul(NM - 1, c, c)
                down_items(BEHIND + 18 * 2 * c // 8, BEHIND + 18 * (2 * c + 1) // 8)
                h_lo(NM - 1, c, c)
                down_items(BEHIND + 18 * (2 * c + 1) // 8, BEHIND + 18 * (2 * c + 2) // 8)

            for t in range(NT):
                d0 = 18 + BEHIND
                down_items(d0 + (CONV_END - d0) * t // NT, d0 + (CONV_END - d0) * (t + 1) // NT)
                dve.wait_ge(conv_done, t + 1)
                dve.wait_ge(xr_ld[t % 4], 16 * (t // 4 + 1))
                v.scalar_tensor_tensor(res[:, t, :], bank[t % 4][:], c_conv, xr[:, t % 4, :],
                                       ALU.mult, ALU.add).then_inc(res_done, 1)
            down_items(CONV_END, 9 * DOWN_LOOP)
            with dve.Fori(DOWN_LOOP // 2, NM // 2) as j:
                for par in range(2):
                    down_unit(2 * j + par, par, NM + 1 + j, 0, 9)
            weight_lo(GU + NM - 1, wd[:, NM - 1, HI, :], wd[:, NM - 1, LO, :])
            for t in range(NT):
                dve.wait_ge(down_done, t + 1)
                v.scalar_tensor_tensor(res[:, t, :], bank[(t + 4) % 8][:], c_down, res[:, t, :],
                                       ALU.mult, ALU.add).then_inc(fin_done, 1)

        @block.tensor
        def _(pe):
            def transpose_tile(t):
                pe.wait_ge(xn_done, t + 1)
                if t >= 4:
                    pe.wait_ge(xlo_done, t - 3)
                for f in range(NC):
                    mm = nc.tensor.transpose(bank[4 + t % 4][:, P * f:P * f + P],
                                             xnb[:, t % 8, P * f:P * f + P], ident[:])
                mm.then_inc(tp_done, 1)

            def products(k, par, c, pair, units=(0, 1)):
                for unit in units:
                    if c == 0:
                        pe.wait_ge(wlo_done, 2 * k + unit + 1)
                    out_b = bank[2 * pair + unit]
                    n = 0
                    for f in range(NC):
                        for wl, xl in ((HI, HI), (HI, LO), (LO, HI)):
                            mm = nc.tensor.matmul(out_b[:], w1[:, par, unit, wl, f, :],
                                                  xT[:, TPC * c:TPC * c + TPC, xl, f, :],
                                                  start=(n == 0), stop=(n == 3 * NC - 1))
                            n += 1
                    mm.then_inc((gate_done, up_done)[unit], 1)

            def first(c, units):
                if c >= 2:
                    pe.wait_ge(hlo_done, c - 1)
                pe.wait_ge(xlo_done, TPC * (c + 1))
                products(0, 0, c, c % 2, units)

            pe.wait_ge(id_done, 2)
            for t in range(0, 8):
                transpose_tile(t)
            first(0, (0,))
            first(1, (0,))
            pe.wait_ge(s4_ld, 48)
            for i in range(2):
                mm = nc.tensor.matmul(bank[3][:, i:i + 1], vcs[:, P * i:P * i + P], bps,
                                      start=True, stop=True)
            mm.then_inc(b_mm, 1)
            for t in range(8, 12):
                transpose_tile(t)
            first(0, (1,))
            pe.wait_ge(b_cp, 1)
            first(1, (1,))
            for t in range(12, 16):
                transpose_tile(t)
            first(2, (0, 1))
            first(3, (0, 1))

            def window(k, par):
                for c in range(NCH):
                    if isinstance(k, int) and k == 1:
                        if c < 2:
                            pe.wait_ge(hlo_done, 3 + c)
                    else:
                        pe.wait_ge(hlo_done, NCH * k + c - 3)
                    if isinstance(k, int) and c == 3:
                        if k == NM - 4:
                            pe.wait_ge(s4_done, SUMS_READ)
                        elif k == NM - 2:
                            pe.wait_ge(t_done, 3)
                    products(k, par, c, c)
                    if isinstance(k, int) and c == 0:
                        if k == NM - 4:
                            s4_sums()
                        elif k == NM - 2:
                            toeplitz()

            def s4_sums():
                pe.wait_ge(hlo_done, NCH * (NM - 4))
                pe.wait_ge(v_done, V_STEPS)
                pe.wait_ge(inv_done, 2)
                for f in range(2):
                    sums, part = bank[6][:, 16 * f:16 * f + 16], slice(P * f, P * f + P)
                    nc.tensor.matmul(sums, e_re[:, part], V_halves[:, 0, :], start=True, stop=False)
                    mm = nc.tensor.matmul(sums, e_im[:, part], V_halves[:, 1, :], start=False, stop=True)
                mm.then_inc(sum_done, 1)

            def toeplitz():
                pe.wait_ge(u_done, 2)
                pe.wait_ge(hlo_done, NCH * (NM - 2))
                terms = (((0, 0), (3, 1)), ((2, 1), (3, 0)), ((2, 0), (1, 1)), ((0, 1), (1, 0)))
                for g, group in enumerate((((0, 0), (2, 0)), ((1, 0), (3, 0)), ((0, 0), (2, 2)), ((1, 1), (3, 3)))):
                    n = 0
                    for a, m in group:
                        for u, cs in terms[m]:
                            mm = nc.tensor.matmul(bank[6][:, P * g:P * g + P], U[u][:, a, :], rhs_t[:, cs, a, :],
                                                  start=(n == 0), stop=(n == 3))
                            n += 1
                mm.then_inc(toe_mm, 1)

            window(1, 1)
            with pe.Fori(2, NM - 5, 2) as k:
                window(k, 0)
                window(k + 1, 1)
            for k in range(NM - 4, NM):
                window(k, k % 2)

            pe.wait_ge(tz_done, 1)
            pe.wait_ge(hlo_done, NCH * NM - 2)
            for t in range(NT):
                if t >= 4:
                    pe.wait_ge(res_done, t - 3)
                n = 0
                for j in range(NC):
                    for xl, tl in ((HI, HI), (HI, LO), (LO, HI)):
                        mm = nc.tensor.matmul(bank[t % 4][:, P * j:HD], xT[:, t, xl, j, :],
                                              tz[:, tl, 0:HD - P * j], start=(n == 0), stop=(n == 3 * NC - 1))
                        n += 1
                mm.then_inc(conv_done, 1)

            def down(mt, t):
                if isinstance(mt, int) and mt == 0:
                    if t == 4:
                        pe.wait_ge(res_done, NT)
                    if t >= 8:
                        pe.wait_ge(fin_done, t - 7)
                for n, (hl, wl) in enumerate(((HI, HI), (HI, LO), (LO, HI))):
                    part = h[:, mt, hl, P * t:P * t + P]
                    if hl == LO:
                        part = part.bitcast(BF16)
                    mm = nc.tensor.matmul(bank[(t + 4) % 8][:], part, wd[:, mt, wl, :],
                                          start=(isinstance(mt, int) and mt == 0 and n == 0),
                                          stop=(isinstance(mt, int) and mt == NM - 1 and n == 2))
                if isinstance(mt, int) and mt == NM - 1:
                    mm.then_inc(down_done, 1)

            pe.wait_ge(hlo_done, NCH * NM)
            for group in range(2):
                tiles = range(8 * group, 8 * group + 8)
                pe.wait_ge(wlo_done, GU + 1)
                for t in tiles:
                    down(0, t)
                rest = NM - 1 if group == 0 else NM - 3
                with pe.Fori(1, rest) as mt:
                    pe.wait_ge(wlo_done, GU + 1 + mt)
                    for t in tiles:
                        down(mt, t)
                pe.wait_ge(wlo_done, GU + NM)
                for t in tiles:
                    for mt in range(rest, NM):
                        down(mt, t)


def _s4_tables(np):
    L = HD
    p, a, f = np.arange(P)[:, None, None], np.arange(4)[None, :, None], np.arange(P)[None, None, :]
    root = 4 * p + a
    rhs = 2 * np.pi * (root * f % L) / L
    lhs = np.pi * (root * (1 - 2 * f) % (2 * L)) / L
    rows = (4 * np.arange(P)[None, :] + np.arange(4)[:, None]).reshape(2, 256) * np.pi / L
    rows = np.repeat(rows, NST, axis=0)
    f32 = np.float32
    return (np.concatenate([np.cos(rows), np.sin(rows)], axis=1).astype(f32),
            np.stack([np.cos(rhs), np.sin(rhs)], axis=1).reshape(P, 2, 4, P).astype(f32),
            (np.stack([np.cos(lhs), np.sin(lhs)], axis=1) / L).reshape(P, 2, 4, P).astype(f32),
            np.cos(root[:, :, 0] * np.pi / L).astype(f32))


def kernel(**inputs):
    import numpy as np
    import concourse.bacc as bacc
    from concourse.bass_utils import run_bass_kernel_spmd

    i = {k: np.asarray(v) for k, v in inputs.items()}

    def gu_codes(q):
        return q.reshape(NM, P, NC, P).transpose(0, 3, 2, 1).reshape(NM, P, HD)

    def gu_absmax(am):
        return am.reshape(NM, P, NC, 2).transpose(0, 3, 2, 1).reshape(NM, 2, HD)

    vc = i["L0_attn_Vc_ri"].transpose(1, 2, 0)
    cols = np.concatenate([i["L0_attn_p_ri"], i["L0_attn_q_ri"], i["L0_attn_Ct_ri"].reshape(NST, 2),
                           i["L0_attn_Lambda_ri"]], axis=1)
    root_rows, tab_rhs, tab_lhs, cos_cols = _s4_tables(np)
    flat = np.stack([i["L0_ffn_gate_absmax"], i["L0_ffn_up_absmax"], i["L0_ffn_down_absmax"]])
    arrays = {
        "x": i["L0_attn_u"],
        "q_gate": gu_codes(i["L0_ffn_gate_q"]),
        "q_up": gu_codes(i["L0_ffn_up_q"]),
        "q_down": i["L0_ffn_down_q"].reshape(HD, NM, P).transpose(1, 2, 0),
        "am_gate": gu_absmax(i["L0_ffn_gate_absmax"]),
        "am_up": gu_absmax(i["L0_ffn_up_absmax"]),
        "am_down": i["L0_ffn_down_absmax"].reshape(HD, NM, 2).transpose(1, 2, 0),
        "am_flat": flat.reshape(3, P, HD * M // 64 // P).transpose(1, 0, 2),
        "s4_cols": np.concatenate([cols, cols], axis=0),
        "vct": np.concatenate([vc, vc], axis=2).reshape(NST, 2 * P),
        "bp": i["L0_attn_Bp"],
        "d_skip": i["L0_attn_D"].reshape(1, 1),
        "log_step": i["L0_attn_log_step"].reshape(1, 1),
        "lines_b": np.tile(np.array([b for _, b in NF4_LINES], np.float32), (P, 1)),
        "root_rows": root_rows,
        "tab_rhs": tab_rhs,
        "tab_lhs": tab_lhs,
        "cos_cols": cos_cols,
    }
    arrays = {f"in_{k}": np.ascontiguousarray(a) for k, a in arrays.items()}

    nc = bacc.Bacc("TRN2", target_bir_lowering=False, num_devices=1)
    args = [nc.dram_tensor(k, a.shape, mybir.dt.from_np(a.dtype), kind="ExternalInput").ap()
            for k, a in arrays.items()]
    args.append(nc.dram_tensor("out_0", i["L0_attn_u"].shape, F32, kind="ExternalOutput").ap())
    ffn_conv_kernel(nc, *args)
    r = run_bass_kernel_spmd(nc, [arrays], core_ids=[0])
    return r.results[0]["out_0"]
```
